# Optimizing a Trainium2 kernel written in Bass

```python
import numpy as np
import jax
import jax.numpy as jnp

def _softmax(x, axis=-1):
    return jax.nn.softmax(x, axis=axis)

def _gelu(x):
    return jax.nn.gelu(x, approximate=True)

def _silu(x):
    return jax.nn.silu(x)

def _sigmoid(x):
    return jax.nn.sigmoid(x)

def _layernorm(x, axis=-1, eps=1e-05):
    m = jnp.mean(x, axis=axis, keepdims=True)
    v = jnp.var(x, axis=axis, keepdims=True)
    return (x - m) / jnp.sqrt(v + eps)

def _scatter_add(tgt, idx, src, axis=0):
    return tgt.at[idx].add(src)

def _segment_sum(src, seg, n):
    return jax.ops.segment_sum(src, seg, n)
kernel_name = 'mk_gnn_preln_d4_gnn_r8_35d8ca'

def setup_inputs(seed: int=0):
    np.random.seed(seed)
    _w = jnp.asarray

    def _rec_inputs():
        import jax
        import jax.numpy as jnp
        _gk = jax.random.key(seed)
        x = -0.0005121 + 1.001 * jax.random.normal(jax.random.fold_in(_gk, 1), (12500, 64), jnp.float32)
        _s = jax.random.randint(jax.random.fold_in(_gk, 2), (100000,), 0, 12500, jnp.int32)
        _d = jax.random.randint(jax.random.fold_in(_gk, 3), (100000,), 0, 12500, jnp.int32)
        _loop = jnp.arange(12500, dtype=jnp.int32)
        src = jnp.concatenate([_s, _d, _loop])
        dst = jnp.concatenate([_d, _s, _loop])
        _o = jnp.argsort(dst, stable=True)
        src = src[_o]
        dst = dst[_o]
        edge_attr_32 = 0.000102155 + 1.00015 * jax.random.normal(jax.random.fold_in(_gk, 13), (212500, 32), jnp.float32)
        return (x, src, dst, edge_attr_32)
    x, src, dst, edge_attr_32 = _rec_inputs()

    def _L0_gnn_setup():
        import jax, jax.numpy as jnp
        import numpy as np
        N, D, H, E = (6250, 64, 4, 100000)
        key = jax.random.key(seed)
        k1, k2, k3, k4, k5 = jax.random.split(key, 5)
        inputs = jax.random.normal(k1, (N, D), dtype=jnp.float32)
        Wh = jax.random.normal(k2, (H, D, D), dtype=jnp.float32) * (1.414 / np.sqrt(D))
        weight = jax.random.normal(k3, (H * D, D), dtype=jnp.float32) * (1.414 / np.sqrt(H * D))
        src = jax.random.randint(k4, (E,), 0, N, dtype=jnp.int64)
        dst = jax.random.randint(k5, (E,), 0, N, dtype=jnp.int64)
        return {'inputs': inputs, 'Wh': Wh, 'weight': weight, 'src': src, 'dst': dst}
    _L0_gnn_all = _L0_gnn_setup()
    _L0_gnn_in = {k: v for k, v in _L0_gnn_all.items() if k in ('Wh', 'weight')}
    del _L0_gnn_all

    def _L1_gnn_setup():
        import jax, jax.numpy as jnp
        import numpy as np
        N, E, D = (12500, 200000, 64)
        key = jax.random.key(seed)
        k1, k2, k3, k4 = jax.random.split(key, 4)
        x = jax.random.normal(k1, (N, D), dtype=jnp.float32)
        edge_index = jax.random.randint(k2, (2, E), 0, N, dtype=jnp.int64)
        W = jax.random.normal(k3, (D, 2 * D), dtype=jnp.float32) * 0.05
        b = jax.random.normal(k4, (D,), dtype=jnp.float32) * 0.05
        return {'x': x, 'edge_index': edge_index, 'W': W, 'b': b}
    _L1_gnn_all = _L1_gnn_setup()
    _L1_gnn_in = {k: v for k, v in _L1_gnn_all.items() if k in ('W', 'b')}
    del _L1_gnn_all

    def _L2_gnn_setup():
        import jax, jax.numpy as jnp
        import numpy as np
        N, E = (6250, 80000)
        IN_DIM, HID, OUT_DIM, HEADS = (64, 128, 64, 8)
        HC = HID // HEADS

        def _p(k, shape, fan_in):
            return jax.random.normal(k, shape, jnp.float32) / np.float32(np.sqrt(fan_in))

        def add_self_loops(ei, n):
            loop = jnp.arange(n, dtype=ei.dtype)
            return jnp.concatenate([ei, jnp.stack([loop, loop])], axis=1)

        def gat_conv(x, ei, W, a_src, a_dst, b, heads, out_ch):
            n = x.shape[0]
            h = (x @ W).reshape(n, heads, out_ch)
            alpha_src = jnp.sum(h * a_src, axis=-1)
            alpha_dst = jnp.sum(h * a_dst, axis=-1)
            src, dst = (ei[0], ei[1])
            e = jax.nn.leaky_relu(alpha_src[src] + alpha_dst[dst], 0.2)
            m = jax.ops.segment_max(e, dst, num_segments=n)
            ex = jnp.exp(e - m[dst])
            s = jax.ops.segment_sum(ex, dst, num_segments=n)
            alpha = ex / (s[dst] + 1e-16)
            out = jax.ops.segment_sum(alpha[:, :, None] * h[src], dst, num_segments=n)
            return out.reshape(n, heads * out_ch) + b
        key = jax.random.key(seed)
        ks = jax.random.split(key, 20)
        x = jax.random.normal(ks[0], (N, IN_DIM), jnp.float32)
        edge_index = jax.random.randint(ks[1], (2, E), 0, N, dtype=jnp.int64)
        return {'x': x, 'edge_index': edge_index, 'W1': _p(ks[2], (IN_DIM, HEADS * HC), IN_DIM), 'as1': _p(ks[3], (HEADS, HC), HC), 'ad1': _p(ks[4], (HEADS, HC), HC), 'b1': jnp.zeros((HEADS * HC,), jnp.float32), 'W2': _p(ks[5], (HID, HEADS * HC), HID), 'as2': _p(ks[6], (HEADS, HC), HC), 'ad2': _p(ks[7], (HEADS, HC), HC), 'b2': jnp.zeros((HEADS * HC,), jnp.float32), 'W3': _p(ks[8], (HID, OUT_DIM), HID), 'as3': _p(ks[9], (1, OUT_DIM), OUT_DIM), 'ad3': _p(ks[10], (1, OUT_DIM), OUT_DIM), 'b3': jnp.zeros((OUT_DIM,), jnp.float32), 'Wp': _p(ks[11], (OUT_DIM, OUT_DIM), OUT_DIM), 'bp': jnp.zeros((OUT_DIM,), jnp.float32)}
    _L2_gnn_all = _L2_gnn_setup()
    _L2_gnn_in = {k: v for k, v in _L2_gnn_all.items() if k in ('W1', 'as1', 'ad1', 'b1', 'W2', 'as2', 'ad2', 'b2', 'W3', 'as3', 'ad3', 'b3', 'Wp', 'bp')}
    del _L2_gnn_all

    def _L3_gnn_setup():
        import jax, jax.numpy as jnp
        import numpy as np
        N_NODES = 12500
        N_EDGES = 125000
        N_GRAPHS = 64
        D_X = 64
        D_EDGE = 32
        H1, O1 = (128, 64)
        H2, O2 = (128, 64)
        key = jax.random.key(seed)
        ks = jax.random.split(key, 16)
        s = 0.05
        return {'x': jax.random.normal(ks[0], (N_NODES, D_X), jnp.float32), 'edge_index': jax.random.randint(ks[1], (2, N_EDGES), 0, N_NODES, jnp.int32), 'edge_attr': jax.random.normal(ks[2], (N_EDGES, D_EDGE), jnp.float32), 'u': jax.random.normal(ks[3], (N_GRAPHS,), jnp.float32), 'batch': jax.random.randint(ks[4], (N_NODES,), 0, N_GRAPHS, jnp.int32), 'W1a': jax.random.normal(ks[5], (D_X + D_EDGE, H1), jnp.float32) * s, 'b1a': jnp.zeros((H1,), jnp.float32), 'W1b': jax.random.normal(ks[6], (H1, H1), jnp.float32) * s, 'b1b': jnp.zeros((H1,), jnp.float32), 'W1c': jax.random.normal(ks[7], (H1, O1), jnp.float32) * s, 'b1c': jnp.zeros((O1,), jnp.float32), 'W2a': jax.random.normal(ks[8], (D_X + O1 + 1, H2), jnp.float32) * s, 'b2a': jnp.zeros((H2,), jnp.float32), 'W2b': jax.random.normal(ks[9], (H2, O2), jnp.float32) * s, 'b2b': jnp.zeros((O2,), jnp.float32)}
    _L3_gnn_all = _L3_gnn_setup()
    _L3_gnn_in = {k: v for k, v in _L3_gnn_all.items() if k in ('u', 'W1a', 'b1a', 'W1b', 'b1b', 'W1c', 'b1c', 'W2a', 'b2a', 'W2b', 'b2b')}
    del _L3_gnn_all
    return {'x': x, 'src': src, 'dst': dst, 'edge_attr_32': edge_attr_32, 'L0_gnn_Wh': _L0_gnn_in['Wh'], 'L0_gnn_weight': _L0_gnn_in['weight'], 'L1_gnn_W': _L1_gnn_in['W'], 'L1_gnn_b': _L1_gnn_in['b'], 'L2_gnn_W1': _L2_gnn_in['W1'], 'L2_gnn_as1': _L2_gnn_in['as1'], 'L2_gnn_ad1': _L2_gnn_in['ad1'], 'L2_gnn_b1': _L2_gnn_in['b1'], 'L2_gnn_W2': _L2_gnn_in['W2'], 'L2_gnn_as2': _L2_gnn_in['as2'], 'L2_gnn_ad2': _L2_gnn_in['ad2'], 'L2_gnn_b2': _L2_gnn_in['b2'], 'L2_gnn_W3': _L2_gnn_in['W3'], 'L2_gnn_as3': _L2_gnn_in['as3'], 'L2_gnn_ad3': _L2_gnn_in['ad3'], 'L2_gnn_b3': _L2_gnn_in['b3'], 'L2_gnn_Wp': _L2_gnn_in['Wp'], 'L2_gnn_bp': _L2_gnn_in['bp'], 'L3_gnn_u': _L3_gnn_in['u'], 'L3_gnn_W1a': _L3_gnn_in['W1a'], 'L3_gnn_b1a': _L3_gnn_in['b1a'], 'L3_gnn_W1b': _L3_gnn_in['W1b'], 'L3_gnn_b1b': _L3_gnn_in['b1b'], 'L3_gnn_W1c': _L3_gnn_in['W1c'], 'L3_gnn_b1c': _L3_gnn_in['b1c'], 'L3_gnn_W2a': _L3_gnn_in['W2a'], 'L3_gnn_b2a': _L3_gnn_in['b2a'], 'L3_gnn_W2b': _L3_gnn_in['W2b'], 'L3_gnn_b2b': _L3_gnn_in['b2b']}

def reference(x, src, dst, edge_attr_32, L0_gnn_Wh, L0_gnn_weight, L1_gnn_W, L1_gnn_b, L2_gnn_W1, L2_gnn_as1, L2_gnn_ad1, L2_gnn_b1, L2_gnn_W2, L2_gnn_as2, L2_gnn_ad2, L2_gnn_b2, L2_gnn_W3, L2_gnn_as3, L2_gnn_ad3, L2_gnn_b3, L2_gnn_Wp, L2_gnn_bp, L3_gnn_u, L3_gnn_W1a, L3_gnn_b1a, L3_gnn_W1b, L3_gnn_b1b, L3_gnn_W1c, L3_gnn_b1c, L3_gnn_W2a, L3_gnn_b2a, L3_gnn_W2b, L3_gnn_b2b):
    import jax
    import jax.numpy as jnp

    def _L0_gnn_ref(inputs, Wh, weight, src, dst):
        import jax, jax.numpy as jnp
        import numpy as np
        N, D, H, E = (6250, 64, 4, 100000)
        n, d = inputs.shape
        h = inputs
        a = jnp.einsum('nd,hde->nhe', h, Wh)
        scores = jnp.sum(a * h[:, None, :], axis=-1) / jnp.sqrt(jnp.asarray(d, h.dtype))
        attn = jax.nn.softmax(scores, axis=0)
        msg = h[src][:, None, :] * attn[src][:, :, None]
        neigh = jax.ops.segment_sum(msg, dst, num_segments=n)
        out = neigh.reshape(n, -1) @ weight
        return jax.nn.elu(out)

    def _L1_gnn_ref(x, edge_index, W, b):
        import jax, jax.numpy as jnp
        import numpy as np
        N, E, D = (12500, 200000, 64)
        row, col = (edge_index[0], edge_index[1])
        msg = jax.nn.relu(jnp.concatenate([x[row], x[col]], axis=-1) @ W.T + b)
        agg = jax.ops.segment_sum(msg, row, num_segments=x.shape[0])
        out = jax.nn.relu(jnp.concatenate([x, agg], axis=-1) @ W.T + b)
        return out

    def _L2_gnn_ref(x, edge_index, W1, as1, ad1, b1, W2, as2, ad2, b2, W3, as3, ad3, b3, Wp, bp):
        import jax, jax.numpy as jnp
        import numpy as np
        N, E = (6250, 80000)
        IN_DIM, HID, OUT_DIM, HEADS = (64, 128, 64, 8)
        HC = HID // HEADS

        def _p(k, shape, fan_in):
            return jax.random.normal(k, shape, jnp.float32) / np.float32(np.sqrt(fan_in))

        def add_self_loops(ei, n):
            loop = jnp.arange(n, dtype=ei.dtype)
            return jnp.concatenate([ei, jnp.stack([loop, loop])], axis=1)

        def gat_conv(x, ei, W, a_src, a_dst, b, heads, out_ch):
            n = x.shape[0]
            h = (x @ W).reshape(n, heads, out_ch)
            alpha_src = jnp.sum(h * a_src, axis=-1)
            alpha_dst = jnp.sum(h * a_dst, axis=-1)
            src, dst = (ei[0], ei[1])
            e = jax.nn.leaky_relu(alpha_src[src] + alpha_dst[dst], 0.2)
            m = jax.ops.segment_max(e, dst, num_segments=n)
            ex = jnp.exp(e - m[dst])
            s = jax.ops.segment_sum(ex, dst, num_segments=n)
            alpha = ex / (s[dst] + 1e-16)
            out = jax.ops.segment_sum(alpha[:, :, None] * h[src], dst, num_segments=n)
            return out.reshape(n, heads * out_ch) + b
        n = x.shape[0]
        ei = add_self_loops(edge_index, n)
        h = gat_conv(x, ei, W1, as1, ad1, b1, HEADS, HC)
        h = jax.nn.elu(h)
        h = gat_conv(h, ei, W2, as2, ad2, b2, HEADS, HC)
        h = jax.nn.elu(h)
        h = gat_conv(h, ei, W3, as3, ad3, b3, 1, OUT_DIM)
        h = h @ Wp + bp
        nrm = jnp.linalg.norm(h, axis=-1, keepdims=True)
        return h / jnp.maximum(nrm, 1e-12)

    def _L3_gnn_ref(x, edge_index, edge_attr, u, batch, W1a, b1a, W1b, b1b, W1c, b1c, W2a, b2a, W2b, b2b):
        import jax, jax.numpy as jnp
        import numpy as np
        N_NODES = 12500
        N_EDGES = 125000
        N_GRAPHS = 64
        D_X = 64
        D_EDGE = 32
        H1, O1 = (128, 64)
        H2, O2 = (128, 64)
        sender, receiver = (edge_index[0], edge_index[1])
        agg = jnp.concatenate([x[sender], edge_attr], axis=1)
        h = jax.nn.relu(agg @ W1a + b1a)
        h = jax.nn.relu(h @ W1b + b1b)
        upd = h @ W1c + b1c
        n = x.shape[0]
        sums = jax.ops.segment_sum(upd, receiver, num_segments=n)
        cnt = jax.ops.segment_sum(jnp.ones((upd.shape[0], 1), upd.dtype), receiver, num_segments=n)
        out = sums / jnp.maximum(cnt, 1.0)
        u_col = u.reshape(-1, 1)
        agg2 = jnp.concatenate([x, out, u_col[batch]], axis=1)
        h2 = jax.nn.relu(agg2 @ W2a + b2a)
        return h2 @ W2b + b2b
    edge_index = jnp.stack([src, dst])
    batch0 = jnp.zeros((12500,), jnp.int32)
    h = jnp.maximum(_layernorm(x, axis=-1), 0.0)
    x = x + _L0_gnn_ref(h, L0_gnn_Wh, L0_gnn_weight, src, dst)
    h = jnp.maximum(_layernorm(x, axis=-1), 0.0)
    x = x + _L1_gnn_ref(h, edge_index, L1_gnn_W, L1_gnn_b)
    h = jnp.maximum(_layernorm(x, axis=-1), 0.0)
    x = x + _L2_gnn_ref(h, edge_index, L2_gnn_W1, L2_gnn_as1, L2_gnn_ad1, L2_gnn_b1, L2_gnn_W2, L2_gnn_as2, L2_gnn_ad2, L2_gnn_b2, L2_gnn_W3, L2_gnn_as3, L2_gnn_ad3, L2_gnn_b3, L2_gnn_Wp, L2_gnn_bp)
    h = jnp.maximum(_layernorm(x, axis=-1), 0.0)
    x = x + _L3_gnn_ref(h, edge_index, edge_attr_32, L3_gnn_u, batch0, L3_gnn_W1a, L3_gnn_b1a, L3_gnn_W1b, L3_gnn_b1b, L3_gnn_W1c, L3_gnn_b1c, L3_gnn_W2a, L3_gnn_b2a, L3_gnn_W2b, L3_gnn_b2b)
    return x

_drawn_inputs = setup_inputs


def setup_inputs(seed=0):
    import zlib

    import numpy as np

    out = dict(_drawn_inputs(seed))
    spreads = {'L2_gnn_b1': (0.0, 2.0),
     'L2_gnn_b2': (0.0, 2.0),
     'L2_gnn_b3': (0.0, 2.0),
     'L2_gnn_bp': (0.0, 2.0),
     'L3_gnn_b1a': (0.0, 0.8),
     'L3_gnn_b1b': (0.0, 2.0),
     'L3_gnn_b1c': (0.0, 2.0),
     'L3_gnn_b2a': (0.0, 2.0),
     'L3_gnn_b2b': (0.0, 0.8)}
    factors = {'edge_attr_32': 8.0,
     'L0_gnn_Wh': 33.954,
     'L0_gnn_weight': 33.672,
     'L2_gnn_as1': 200.0,
     'L2_gnn_ad1': 200.0,
     'L2_gnn_as2': 200.0,
     'L2_gnn_ad2': 200.0,
     'L2_gnn_as3': 200.0,
     'L2_gnn_ad3': 200.0,
     'L3_gnn_u': 35.688,
     'L3_gnn_W1a': 8.0,
     'L3_gnn_W1b': 8.0,
     'L3_gnn_W1c': 7.139,
     'L1_gnn_b': 2.918,
     'L2_gnn_W1': 64.0,
     'L2_gnn_W2': 45.682,
     'L2_gnn_W3': 36.463,
     'L2_gnn_Wp': 21.196}
    for name, (base, spread) in spreads.items():
        noise = np.random.default_rng([zlib.crc32(name.encode()), seed]).standard_normal(out[name].shape)
        drawn = base * np.exp(spread * noise) if base else spread * noise
        out[name] = jnp.asarray(drawn.astype(out[name].dtype))
    for name, factor in factors.items():
        out[name] = (out[name] * factor).astype(out[name].dtype)
    return out
```

```python
from contextlib import ExitStack

import numpy as np
import concourse.bass as bass
from concourse import mybir

F32 = mybir.dt.float32
BF16 = mybir.dt.bfloat16
I32 = mybir.dt.int32
ALU = mybir.AluOpType
ACT = mybir.ActivationFunctionType
AX = mybir.AxisListType

P = 128
N = 12500
E = 212500
D = 64
DE = 32
NT = -(-N // P)
NP = NT * P
GT = 16
GROUP = GT * P
NG = -(-E // (2 * GROUP)) * 2
IT = NG // 2
T = NG * GT
EP = T * P
TB = T // P
ROW = 2 + DE
HEADS, CH = 8, 16
H0 = 4
BIG = 1.0e38
SKIP = 1 << 20
EPS = 1e-5
RMAX, RADD = bass.bass_isa.ReduceOp.max, bass.bass_isa.ReduceOp.add
QT = 4
assert T % P == 0 and N < P * P


class Signal:

    def __init__(self, phase, name, engine, per_iter=0, inc=1, credit=0):
        self.sem = phase.sem(name)
        self.per_iter, self.inc, self.credit = per_iter, inc, credit
        self.ahead = credit
        if credit and engine and inc == 1:
            phase.on(engine, lambda e: e.sem_inc(self.sem, credit))
        elif credit and engine:
            self.ahead = 16
            to, of = phase.prime()
            phase.on(engine, lambda e: e.dma_start(to, of).then_inc(self.sem, 16))

    def mark(self, instruction):
        instruction.then_inc(self.sem, self.inc)

    def wait(self, e, it, n):
        assert n + self.credit >= 1
        e.wait_ge(self.sem, it * (self.per_iter * self.inc) + (n * self.inc + self.ahead))


class Phase:

    def __init__(self, nc, name, prime_source=None):
        self.nc, self.name, self.prime_source = nc, name, prime_source
        self.stack = ExitStack()
        self.sems = []
        self.work = {k: [] for k in ("sync", "gpsimd", "scalar", "tensor", "vector")}

    def sb(self, name, shape, dt=F32):
        return self.stack.enter_context(self.nc.sbuf_tensor(f"{self.name}_{name}", shape, dt))

    def ps(self, name, shape, dt=F32):
        return self.stack.enter_context(self.nc.psum_tensor(f"{self.name}_{name}", shape, dt))

    def sem(self, name):
        s = self.nc.alloc_semaphore(f"{self.name}_{name}")
        self.sems.append(s)
        return s

    def prime(self):
        to = self.nc.dram_tensor(f"{self.name}_prime{len(self.sems)}", (16, 1), F32, kind="Internal").ap()
        return to, self.prime_source[0:16, 0:1]

    def on(self, engine, program):
        self.work[engine].append(program)

    def run(self, keep=False):
        with self.nc.allow_non_contiguous_dma(reason="small strided tables"), self.nc.Block() as block:
            for engine, programs in self.work.items():
                def body(e, programs=programs):
                    for program in programs:
                        program(e)
                if programs:
                    dict(sync=block.sync, gpsimd=block.gpsimd, scalar=block.scalar,
                         tensor=block.tensor, vector=block.vector)[engine](body)
        self.nc.clear_and_free_semaphores(self.sems)
        self.nc.all_engine_barrier()
        if not keep:
            self.stack.close()


class Chain:

    def __init__(self, phase, name="chain"):
        self.phase, self.name, self.sem, self.total, self.dmas = phase, name, phase.sem(name), 0, 0
        self.now = None

    def step(self, engine, program, count=1, dma=False):
        before = self.now
        if dma:
            sem, inc = self.phase.sem(f"{self.name}_dma{self.dmas}"), 16
            self.dmas += 1
            self.now = (sem, count * inc)
        else:
            sem, inc = self.sem, 1
            self.total += count
            self.now = (sem, self.total)

        def emit(e):
            if before:
                e.wait_ge(*before)
            done = program(e)
            done = done if isinstance(done, list) else [done]
            assert len(done) == count
            for instruction in done:
                instruction.then_inc(sem, inc)
        self.phase.on(engine, emit)

    def v(self, program, count=1):
        self.step("vector", program, count)

    def a(self, program, count=1):
        self.step("scalar", program, count)

    def g(self, program, count=1):
        self.step("gpsimd", program, count)

    def load(self, program, count=1):
        self.step("sync", program, count, dma=True)

    def indirect(self, program, count=1):
        self.step("gpsimd", program, count, dma=True)

    def finish(self, engine="sync"):
        last = self.now
        self.phase.on(engine, lambda e: e.wait_ge(*last))


def gather(e, out, table, index, bound=None):
    kw = {} if bound is None else dict(bounds_check=bound, oob_is_err=False)
    return e.indirect_dma_start(out, None, table, bass.IndirectOffsetOnAxis(ap=index, axis=0), **kw)


def scatter(e, table, index, rows, bound=None):
    kw = {} if bound is None else dict(bounds_check=bound, oob_is_err=False)
    return e.indirect_dma_start(table, bass.IndirectOffsetOnAxis(ap=index, axis=0), rows, None, **kw)


def over(ap, n):
    return ap.unsqueeze(len(ap.shape)).to_broadcast([*ap.shape, n])


def row_numbers(c, out, pos, tmp):
    c.v(lambda e: [
        e.tensor_scalar(out, pos, 0x7FFFFFFF ^ (GROUP - 1), None, ALU.bitwise_and),
        e.tensor_scalar(tmp, pos, P - 1, 4, ALU.bitwise_and, ALU.logical_shift_left)], 2)
    c.v(lambda e: e.tensor_tensor(out, out, tmp, ALU.bitwise_or))
    c.v(lambda e: e.tensor_scalar(tmp, pos, 7, GT - 1, ALU.logical_shift_right, ALU.bitwise_and))
    c.v(lambda e: e.tensor_tensor(out, out, tmp, ALU.bitwise_or))


class Kernel:
    def __init__(self, nc, ins, out):
        self.nc, self.ins, self.out = nc, ins, out
        self.top = ExitStack()

    def sb(self, name, shape, dt=F32):
        return self.top.enter_context(self.nc.sbuf_tensor(name, shape, dt))

    def dram(self, name, shape, dt=F32):
        return self.nc.dram_tensor(name, shape, dt, kind="Internal").ap()

    def constants(self):
        self.x = self.sb("x", [P, NT, D])
        self.feat = self.sb("feat", [P, NT, 2 * D])
        self.ident = self.sb("ident", [P, P])
        self.below = self.sb("below", [P, P])
        self.above = self.sb("above", [P, P])
        self.iota_free = self.sb("iota_free", [P, P], BF16)
        self.iota_part = self.sb("iota_part", [P, 1])
        self.end_row = self.sb("end_row", [P, 2, NT], I32)
        self.start_row = self.sb("start_row", [P, 2, NT], I32)
        self.count = self.sb("count", [P, 2, NT])
        self.first_key = self.sb("first_key", [P, 2, TB], I32)
        self.patch_row = self.sb("patch_row", [P, 2, TB], I32)
        self.first_row = self.sb("first_row", [P, TB], I32)
        self.start_pos = self.sb("start_pos", [P, 2, P])
        self.links = self.sb("links", [P, 2, T], BF16)
        self.sorted_d = self.dram("sorted_d", (EP, ROW), I32)
        self.sorted_s = self.dram("sorted_s", (EP, 2), I32)
        self.pairs_d = self.dram("pairs_d", (EP, 2), I32)
        ph = Phase(self.nc, "const")
        iota_i = ph.sb("iota_i", [P, P], I32)
        c = Chain(ph)
        c.load(lambda e: e.dma_start(self.x[:, :, :], self.ins["x"].rearrange("(p t) d -> p t d", t=NT)))
        c.g(lambda e: [e.memset(self.ident[:, :], 0.0), e.memset(self.below[:, :], 1.0),
                       e.memset(self.above[:, :], 1.0),
                       e.iota(iota_i[:, :], [[1, P]], base=0, channel_multiplier=0)], 4)
        c.v(lambda e: e.tensor_copy(self.iota_free[:, :], iota_i[:, :]))
        c.g(lambda e: [
            e.affine_select(out=self.ident[:, :], in_=self.ident[:, :], compare_op=ALU.not_equal, fill=1.0,
                            base=0, pattern=[[-1, P]], channel_multiplier=1),
            e.affine_select(out=self.below[:, :], in_=self.below[:, :], compare_op=ALU.is_gt, fill=0.0,
                            base=0, pattern=[[-1, P]], channel_multiplier=1),
            e.affine_select(out=self.above[:, :], in_=self.above[:, :], compare_op=ALU.is_gt, fill=0.0,
                            base=0, pattern=[[1, P]], channel_multiplier=-1),
            e.iota(iota_i[:, 0:1], [[0, 1]], base=0, channel_multiplier=1)], 4)
        c.v(lambda e: e.tensor_copy(self.iota_part[:, :], iota_i[:, 0:1]))
        tile = ph.sb("tile", [P, TB], I32)
        tmp = ph.sb("tmp", [P, TB], I32)
        c.g(lambda e: e.iota(tile[:, :], [[P, TB]], base=0, channel_multiplier=1))
        c.v(lambda e: [e.tensor_scalar(self.first_row[:, :], tile[:, :], 4, 11, ALU.logical_shift_right,
                                       ALU.logical_shift_left),
                       e.tensor_scalar(tmp[:, :], tile[:, :], GT - 1, None, ALU.bitwise_and)], 2)
        c.v(lambda e: e.tensor_tensor(self.first_row[:, :], self.first_row[:, :], tmp[:, :], ALU.bitwise_or))
        c.finish()
        ph.run()

    def histogram(self):
        ph = Phase(self.nc, "hist")
        raw = [ph.sb(f"raw{k}", [P, 2, GT], I32) for k in range(2)]
        part = [ph.sb(f"part{k}", [P, 2, 2, GT], I32) for k in range(2)]
        part_f = [ph.sb(f"part_f{k}", [P, 2, 2, GT]) for k in range(2)]
        RING = 4
        hot = [ph.sb(f"hot{k}", [P, 2, 2, P], BF16) for k in range(RING)]
        zero = ph.sb("zero", [P, 2 * P], BF16)
        ps = ph.ps("ps", [P, 2, P])
        loaded = [Signal(ph, f"loaded{k}", "sync", 1, 32) for k in range(2)]
        ints = Signal(ph, "ints", "vector", 4)
        split = Signal(ph, "split", "vector", 2, credit=2)
        hots = Signal(ph, "hots", "vector", 2 * GT)
        summed = Signal(ph, "summed", "tensor", 2 * GT, credit=RING)
        opened = Signal(ph, "opened", "tensor")
        z = Signal(ph, "z", "vector")
        keys = [self.ins["dst"], self.ins["src"]]

        def loads(e):
            with e.Fori(0, IT) as it:
                for k in range(2):
                    split.wait(e, it, k - 1)
                    for s in range(2):
                        e.dma_start(raw[k][:, s, :], keys[s][bass.ds(it * 2 + k, 1), :, :]
                                    .rearrange("g p t -> (g p) t")).then_inc(loaded[k].sem, 16)
        ph.on("sync", loads)

        def dve(e):
            z.mark(e.memset(zero[:, :], 0.0))
            with e.Fori(0, IT) as it:
                for k in range(2):
                    loaded[k].wait(e, it, 1)
                    e.tensor_scalar(part[k][:, 0], raw[k][:, :, :], 7, None, ALU.logical_shift_right).then_inc(ints.sem, 1)
                    e.tensor_scalar(part[k][:, 1], raw[k][:, :, :], P - 1, None, ALU.bitwise_and).then_inc(ints.sem, 1)
                    ints.wait(e, it, 2 * k + 2)
                    split.mark(e.tensor_copy(part_f[k][:, :, :, :], part[k][:, :, :, :]))
                    split.wait(e, it, k + 1)
                    for t in range(GT):
                        s = k * GT + t
                        summed.wait(e, it, s + 1 - RING)
                        for a in range(2):
                            for key in range(2):
                                last = e.tensor_scalar(hot[s % RING][:, a, key, :], self.iota_free[:, :],
                                                       part_f[k][:, a, key, t:t + 1], None, ALU.is_equal)
                        hots.mark(last)
        ph.on("vector", dve)

        def pe(e):
            z.wait(e, 0, 1)
            e.matmul(ps[:, :, :], zero[:, 0:P], zero[:, :], start=True, stop=False)
            with e.Fori(0, IT) as it:
                for s in range(2 * GT):
                    hots.wait(e, it, s + 1)
                    for key in range(2):
                        last = e.matmul(ps[:, key, :], hot[s % RING][:, 0, key, :], hot[s % RING][:, 1, key, :],
                                        start=False, stop=False)
                    summed.mark(last)
            opened.mark(e.matmul(ps[:, :, :], zero[:, 0:P], zero[:, :], start=False, stop=True))
        ph.on("tensor", pe)

        c = Chain(ph)
        cnt = ph.sb("cnt", [P, 2, P])
        incl = ph.sb("incl", [P, 2, P])
        ones = ph.sb("ones", [P, P])
        off_ps = ph.ps("off_ps", [P, 2])
        off = ph.sb("off", [P, 2])
        pos = ph.sb("pos", [P, 2, 2, P])
        pos_i = ph.sb("pos_i", [P, 2, 2, P], I32)
        span = ph.sb("span", [P, 2, P, 2], I32)
        rows = ph.sb("rows", [P, 2, 2, P], I32)
        tmp = ph.sb("tmp", [P, 2, 2, P], I32)
        row_f = ph.sb("row_f", [P, 2, 2, P])
        empty = ph.sb("empty", [P, 2, P])
        aligned = ph.sb("aligned", [P, 2, P], I32)
        aligned_f = ph.sb("aligned_f", [P, 2, P])
        ph.on("vector", lambda e: opened.wait(e, 0, 1))
        c.v(lambda e: [e.tensor_copy(cnt[:, :, :], ps[:, :, :]), e.memset(ones[:, :], 1.0)], 2)
        c.v(lambda e: [e.tensor_tensor_scan(incl[:, s, :], ones[:, :], cnt[:, s, :], 0.0, ALU.mult, ALU.add)
                       for s in range(2)], 2)
        c.step("tensor", lambda e: e.matmul(off_ps[:, :], self.above[:, :], incl[:, :, P - 1], start=True, stop=True))
        c.v(lambda e: e.tensor_copy(off[:, :], off_ps[:, :]))
        c.v(lambda e: [e.tensor_scalar(pos[:, 1, s, :], incl[:, s, :], off[:, s:s + 1], -1.0, ALU.add, ALU.add)
                       for s in range(2)], 2)
        c.v(lambda e: [e.scalar_tensor_tensor(pos[:, 0, s, :], incl[:, s, :], off[:, s:s + 1], cnt[:, s, :],
                                              ALU.add, ALU.subtract) for s in range(2)], 2)
        c.v(lambda e: [e.tensor_copy(self.start_pos[:, :, :], pos[:, 0]), e.tensor_copy(pos_i[:, :, :, :], pos[:, :, :, :]),
                       e.tensor_copy(span[:, :, :, 0], pos[:, 0]), e.tensor_copy(span[:, :, :, 1], pos[:, 1]),
                       e.tensor_scalar(empty[:, :, :], cnt[:, :, :], 0.0, float(SKIP), ALU.is_equal, ALU.mult)], 5)
        row_numbers(c, rows[:, :, :, :], pos_i[:, :, :, :], tmp[:, :, :, :])
        c.v(lambda e: [e.tensor_copy(row_f[:, :, :, :], rows[:, :, :, :]),
                       e.tensor_scalar(aligned[:, :, :], pos_i[:, 0], P - 1, None, ALU.bitwise_and)], 2)
        c.v(lambda e: e.tensor_copy(aligned_f[:, :, :], aligned[:, :, :]))
        c.v(lambda e: e.tensor_scalar(aligned_f[:, :, :], aligned_f[:, :, :], 0.0, float(SKIP), ALU.is_equal, ALU.mult))
        c.v(lambda e: [e.tensor_tensor(row_f[:, s], row_f[:, s], empty[:, :, :], ALU.add) for s in range(2)], 2)
        c.v(lambda e: e.tensor_tensor(row_f[:, 0], row_f[:, 0], aligned_f[:, :, :], ALU.add))
        c.v(lambda e: e.tensor_copy(rows[:, :, :, :], row_f[:, :, :, :]))
        self.span = [self.dram(f"span{s}", (NP, 2), I32) for s in range(2)]
        row_tab = self.dram("row_tab", (2, 2, NP), I32)
        cnt_tab = self.dram("cnt_tab", (2, NP))

        def by_node(a):
            return a.rearrange("(h l) -> h l", l=P)
        c.load(lambda e: [e.dma_start(self.span[s].rearrange("(h l) a -> h l a", l=P), span[0:NT, s, :, :]) for s in range(2)]
               + [e.dma_start(by_node(row_tab[a, s, :]), rows[0:NT, a, s, :]) for a in range(2) for s in range(2)]
               + [e.dma_start(by_node(cnt_tab[s, :]), cnt[0:NT, s, :]) for s in range(2)], 8)
        c.load(lambda e: [e.dma_start(self.start_row[:, s, :], row_tab[0, s, :].rearrange("(p t) -> p t", t=NT)) for s in range(2)]
               + [e.dma_start(self.end_row[:, s, :], row_tab[1, s, :].rearrange("(p t) -> p t", t=NT)) for s in range(2)]
               + [e.dma_start(self.count[:, s, :], cnt_tab[s, :].rearrange("(p t) -> p t", t=NT)) for s in range(2)], 6)
        c.finish()
        ph.run()

    def sort(self):
        ph = Phase(self.nc, "sort", self.ident)
        B2 = range(2)
        raw = [ph.sb(f"raw{k}", [P, 2, GT], I32) for k in B2]
        row_d = [ph.sb(f"row_d{k}", [P, GT, ROW], I32) for k in B2]
        row_s = [ph.sb(f"row_s{k}", [P, GT, 2], I32) for k in B2]
        part = [ph.sb(f"part{k}", [P, 2, 2, GT], I32) for k in B2]
        num = [ph.sb(f"num{k}", [P, 3, 2, GT]) for k in B2]
        hot = [ph.sb(f"hot{k}", [P, 2, 2, P], BF16) for k in B2]
        hot_t = [ph.sb(f"hot_t{k}", [P, 2, P]) for k in B2]
        table = [ph.sb(f"table{k}", [P, 2, P]) for k in B2]
        junk = [ph.sb(f"junk{k}", [P, 4, P]) for k in B2]
        rank = [ph.sb(f"rank{k}", [P, 2, GT]) for k in B2]
        base = [ph.sb(f"base{k}", [P, 2, GT]) for k in B2]
        pos = [ph.sb(f"pos{k}", [P, 2, GT], I32) for k in B2]
        dest = [ph.sb(f"dest{k}", [P, 2, GT], I32) for k in B2]
        tmp = [ph.sb(f"tmp{k}", [P, 2, GT], I32) for k in B2]
        ps_bc = [ph.ps(f"ps_bc{k}", [P, 2, 2, P]) for k in B2]
        ps_look = [ph.ps(f"ps_look{k}", [P, 2, P]) for k in B2]
        ps_table = ph.ps("ps_table", [P, 2, P])
        U = 2 * GT
        loaded = [Signal(ph, f"loaded{k}", "sync", 1, 48) for k in B2]
        ints = Signal(ph, "ints", "vector", 4)
        split = Signal(ph, "split", "vector", 2, credit=2)
        filled = Signal(ph, "filled", "vector", 2)
        bcast = Signal(ph, "bcast", "tensor", U)
        bc_read = Signal(ph, "bc_read", "vector", U, credit=2)
        hotted_t = Signal(ph, "hotted_t", "vector", U)
        hotted = Signal(ph, "hotted", "vector", U)
        looked = Signal(ph, "looked", "tensor", U, credit=2)
        look_read = Signal(ph, "look_read", "vector", U, credit=2)
        updated = Signal(ph, "updated", "tensor", U, credit=2)
        tabled = Signal(ph, "tabled", None, U, credit=1)
        numbers = Signal(ph, "numbers", "vector", 14)
        placed = Signal(ph, "placed", "vector", 2)
        moved = [Signal(ph, f"moved{k}", "gpsimd", 1, 32 * 16, credit=1) for k in B2]
        first = Signal(ph, "first", "tensor")
        table0 = Signal(ph, "table0", "scalar")
        turns = Signal(ph, "turns", "gpsimd")
        keys = [self.ins["dst"], self.ins["src"]]

        def loads(e):
            with e.Fori(0, IT) as it:
                for k in B2:
                    split.wait(e, it, k - 1)
                    moved[k].wait(e, it, 0)
                    for s in range(2):
                        e.dma_start(raw[k][:, s, :], keys[s][bass.ds(it * 2 + k, 1), :, :]
                                    .rearrange("g p t -> (g p) t")).then_inc(loaded[k].sem, 16)
                    e.dma_start(row_d[k][:, :, 2:ROW].bitcast(F32), self.ins["attr"][bass.ds(it * 2 + k, 1), :, :, :]
                                .rearrange("g p t f -> (g p) t f")).then_inc(loaded[k].sem, 16)
        ph.on("sync", loads)

        def values(e, it, s):
            k, t = divmod(s, GT)
            looked.wait(e, it, s + 1)
            hotted.wait(e, it, s + 1)
            look_read.wait(e, it, s - 1)
            for key in range(2):
                last = e.tensor_tensor_reduce(out=junk[s % 2][:, 2 + key, :], in0=ps_look[s % 2][:, key, :], in1=hot[s % 2][:, 1, key, :],
                                              scale=1.0, scalar=0.0, op0=ALU.mult, op1=ALU.add,
                                              accum_out=base[k][:, key, t:t + 1])
            look_read.mark(last)

        def place(e, it, k):
            look_read.wait(e, it, (k + 1) * GT)
            n = [7 * k]

            def do(*ins):
                for i in ins:
                    numbers.mark(i)
                n[0] += len(ins)
                numbers.wait(e, it, n[0])
            moved[k].wait(e, it, 0)
            do(e.tensor_tensor(base[k][:, :, :], base[k][:, :, :], rank[k][:, :, :], ALU.add))
            do(e.tensor_copy(pos[k][:, :, :], base[k][:, :, :]))
            do(e.tensor_scalar(dest[k][:, :, :], pos[k][:, :, :], 0x7FFFFFFF ^ (GROUP - 1), None, ALU.bitwise_and),
               e.tensor_scalar(tmp[k][:, :, :], pos[k][:, :, :], P - 1, 4, ALU.bitwise_and, ALU.logical_shift_left))
            do(e.tensor_tensor(dest[k][:, :, :], dest[k][:, :, :], tmp[k][:, :, :], ALU.bitwise_or))
            do(e.tensor_scalar(tmp[k][:, :, :], pos[k][:, :, :], 7, GT - 1, ALU.logical_shift_right, ALU.bitwise_and))
            do(e.tensor_copy(pos[k][:, :, :], tmp[k][:, :, :]))
            placed.mark(e.tensor_tensor(dest[k][:, :, :], dest[k][:, :, :], pos[k][:, :, :], ALU.bitwise_or))

        def dve(e):
            with e.Fori(0, IT) as it:
                for k in B2:
                    loaded[k].wait(e, it, 1)
                    e.tensor_scalar(part[k][:, 0], raw[k][:, :, :], 7, None, ALU.logical_shift_right).then_inc(ints.sem, 1)
                    e.tensor_scalar(part[k][:, 1], raw[k][:, :, :], P - 1, None, ALU.bitwise_and).then_inc(ints.sem, 1)
                    ints.wait(e, it, 2 * k + 2)
                    e.tensor_copy(num[k][:, 0:2], part[k][:, :, :, :])
                    split.mark(e.tensor_copy(num[k][:, 2], raw[k][:, :, :]))
                    split.wait(e, it, k + 1)
                    moved[k].wait(e, it, 0)
                    e.tensor_copy(row_d[k][:, :, 0], num[k][:, 2, 0])
                    e.tensor_copy(row_d[k][:, :, 1], num[k][:, 2, 1])
                    e.tensor_copy(row_s[k][:, :, 0], num[k][:, 2, 1])
                    filled.mark(e.tensor_copy(row_s[k][:, :, 1], num[k][:, 2, 0]))
                    for t in range(GT):
                        s = k * GT + t
                        bcast.wait(e, it, s + 1)
                        looked.wait(e, it, s - 1)
                        hotted_t.mark(e.tensor_scalar(hot_t[s % 2][:, :, :], ps_bc[s % 2][:, 0], self.iota_part[:, :], None,
                                                      ALU.is_equal))
                        bc_read.wait(e, it, s - 1)
                        for key in range(2):
                            last = e.scalar_tensor_tensor(
                                junk[s % 2][:, key, :], ps_bc[s % 2][:, 1, key, :], num[k][:, 2, key, t:t + 1], self.below[:, :],
                                ALU.is_equal, ALU.mult, accum_out=rank[k][:, key, t:t + 1])
                        bc_read.mark(last)
                        updated.wait(e, it, s - 1)
                        look_read.wait(e, it, s - 1)
                        for a in range(2):
                            for key in range(2):
                                last = e.tensor_scalar(hot[s % 2][:, a, key, :], self.iota_free[:, :],
                                                       num[k][:, a, key, t:t + 1], None, ALU.is_equal)
                        hotted.mark(last)
                        if s % GT:
                            values(e, it, s - 1)
                    values(e, it, k * GT + GT - 1)
                    place(e, it, k)
        ph.on("vector", dve)

        def pe(e):
            first.mark(e.matmul(ps_table[:, :, :], self.ident[:, :], self.start_pos[:, :, :], start=True, stop=True))

            def spread(it, s):
                k, t = divmod(s, GT)
                if t == 0:
                    split.wait(e, it, k + 1)
                bc_read.wait(e, it, s - 1)
                for a, what in ((0, 0), (1, 2)):
                    for key in range(2):
                        last = e.transpose(ps_bc[s % 2][:, a, key, :], num[k][:, what, key, t:t + 1].to_broadcast([P, P]),
                                           self.ident[:, :])
                bcast.mark(last)
            with e.Fori(0, IT) as it:
                for s in range(U):
                    if s % GT == 0:
                        spread(it, s)
                    if (s + 1) % GT:
                        spread(it, s + 1)
                    hotted_t.wait(e, it, s + 1)
                    tabled.wait(e, it, s)
                    look_read.wait(e, it, s - 1)
                    for key in range(2):
                        last = e.matmul(ps_look[s % 2][:, key, :], hot_t[s % 2][:, key, :], table[s % 2][:, key, :],
                                        start=True, stop=True)
                    looked.mark(last)
                    hotted.wait(e, it, s + 1)
                    for key in range(2):
                        last = e.matmul(ps_table[:, key, :], hot[s % 2][:, 0, key, :], hot[s % 2][:, 1, key, :],
                                        start=False, stop=True, skip_group_check=True)
                    updated.mark(last)
        ph.on("tensor", pe)

        def act(e):
            first.wait(e, 0, 1)
            table0.mark(e.activation(table[0][:, :, :], ps_table[:, :, :], ACT.Copy))
            table0.wait(e, 0, 1)
            e.sem_inc(tabled.sem, 1)
            with e.Fori(0, IT) as it:
                for s in range(U):
                    updated.wait(e, it, s + 1)
                    tabled.mark(e.activation(table[(s + 1) % 2][:, :, :], ps_table[:, :, :], ACT.Copy))
        ph.on("scalar", act)

        def pool(e):
            with e.Fori(0, IT) as it:
                for k in B2:
                    filled.wait(e, it, k + 1)
                    placed.wait(e, it, k + 1)
                    e.sem_inc(turns.sem, 1)
                    for t in range(GT):
                        scatter(e, self.sorted_d, dest[k][:, 0, t:t + 1], row_d[k][:, t, :]).then_inc(moved[k].sem, 16)
                        scatter(e, self.sorted_s, dest[k][:, 1, t:t + 1], row_s[k][:, t, :]).then_inc(moved[k].sem, 16)
            for k in B2:
                moved[k].wait(e, 0, IT)
        ph.on("gpsimd", pool)
        ph.run()



    def boundaries(self):
        ph = Phase(self.nc, "bound")
        c = Chain(ph)
        by_tile = ph.sb("by_tile", [NG, 2, 2, GT], I32)
        last = ph.sb("last", [P, 2, T], I32)
        last_f = ph.sb("last_f", [P, 2, T])
        spans = ph.sb("spans", [P, 2, TB, 2], I32)
        span_f = ph.sb("span_f", [P, 2, TB, 2])
        end_i = ph.sb("end_i", [P, 2, TB], I32)
        row = ph.sb("row", [P, 2, TB], I32)
        tmp = ph.sb("tmp", [P, 2, TB], I32)
        row_f = ph.sb("row_f", [P, 2, TB])
        begin = ph.sb("begin", [P, 2, TB])
        begin_i = ph.sb("begin_i", [P, 2, TB], I32)
        no = ph.sb("no", [P, 2, 2, TB])
        tile_key = self.dram("tile_key", (2, 2, T), I32)
        tables = [self.sorted_d, self.sorted_s]
        c.load(lambda e: [e.dma_start(by_tile[:, a, s, :], tables[s].rearrange("(g p t) c -> g p t c", p=P, t=GT)[:, a * (P - 1), :, 0])
                          for a in range(2) for s in range(2)], 4)
        c.load(lambda e: [e.dma_start(tile_key[a, s, :].rearrange("(g t) -> g t", t=GT), by_tile[:, a, s, :])
                          for a in range(2) for s in range(2)], 4)
        c.load(lambda e: [e.dma_start(self.first_key[:, s, :], tile_key[0, s, :].rearrange("(b q) -> q b", q=P)) for s in range(2)]
               + [e.dma_start(last[:, s, :], tile_key[1, s:s + 1, :].to_broadcast([P, T])) for s in range(2)], 4)
        c.v(lambda e: [e.tensor_copy(last_f[:, :, :], last[:, :, :]), e.memset(self.links[:, :, 0:1], 0.0)], 2)
        c.v(lambda e: e.tensor_tensor(self.links[:, :, 1:T], last_f[:, :, 1:T], last_f[:, :, 0:T - 1], ALU.is_equal))
        c.indirect(lambda e: [gather(e, spans[:, s, b, :], self.span[s][:, :], self.first_key[:, s, b:b + 1])
                              for s in range(2) for b in range(TB)], 2 * TB)
        c.g(lambda e: [e.iota(begin_i[:, s, :], [[P * P, TB]], base=0, channel_multiplier=P) for s in range(2)], 2)
        c.v(lambda e: [e.tensor_copy(span_f[:, :, :, :], spans[:, :, :, :]), e.tensor_copy(end_i[:, :, :], spans[:, :, :, 1]),
                       e.tensor_copy(begin[:, :, :], begin_i[:, :, :])], 3)
        row_numbers(c, row[:, :, :], end_i[:, :, :], tmp[:, :, :])
        c.v(lambda e: [e.tensor_copy(row_f[:, :, :], row[:, :, :]),
                       e.tensor_tensor(no[:, 0], span_f[:, :, :, 0], begin[:, :, :], ALU.is_ge),
                       e.tensor_tensor(no[:, 1], span_f[:, :, :, 1], begin[:, :, :], ALU.subtract)], 3)
        c.v(lambda e: e.tensor_scalar(no[:, 1], no[:, 1], float(P), None, ALU.is_ge))
        c.v(lambda e: e.tensor_tensor(no[:, 0], no[:, 0], no[:, 1], ALU.add))
        c.v(lambda e: e.scalar_tensor_tensor(row_f[:, :, :], no[:, 0], float(SKIP), row_f[:, :, :], ALU.mult, ALU.add))
        c.v(lambda e: e.tensor_copy(self.patch_row[:, :, :], row_f[:, :, :]))
        c.finish()
        ph.run()

    def edge_pass(self, name, kind, s, table, out, last, values=None, heads=1, ch=D, weights=None):
        ph = Phase(self.nc, name, self.ident)
        B2, QUADS = range(2), GT // QT
        U = 2 * QUADS
        gat, attr, mlp = kind == "gat", kind == "attr", kind == "mlp"
        HF = heads * ch
        FG = HF + heads if gat else HF
        FO = HF + 2 * heads if gat else HF
        FV = 0 if values is None else values.shape[1]
        from_rows = kind in ("sum", "attr")
        RW = ROW if from_rows else 2
        source = self.sorted_d if from_rows else (self.pairs_d if s == 0 else self.sorted_s)
        source = source.rearrange("(g p t) c -> g p t c", p=P, t=GT)
        out_v = out.rearrange("(g p t) c -> g p t c", p=P, t=GT)
        last_v = last.rearrange("(g t) c -> g t c", t=GT)

        rows = [ph.sb(f"rows{k}", [P, GT, RW], I32) for k in B2]
        key = [ph.sb(f"key{k}", [P, GT]) for k in B2]
        got = [ph.sb(f"got{k}", [P, GT, FG]) for k in B2]
        equal = [ph.sb(f"equal{k}", [P, GT, P]) for k in B2]
        outs = [ph.sb(f"outs{k}", [P, GT, FO]) for k in B2]
        PW = 256 if FG > P else P
        ps_key = [ph.ps(f"ps_key{k}", [P, QT, P]) for k in B2]
        ps_sum = [ph.ps(f"ps_sum{k}", [P, QT, PW]) for k in B2]
        stores = 3 if kind == "sum" else 2
        loaded = [Signal(ph, f"loaded{k}", "sync", 1, 16 * (1 + (FV > 0))) for k in B2]
        gathered = [Signal(ph, f"gathered{k}", "gpsimd", 1, 16 * GT) for k in B2]
        stored = [Signal(ph, f"stored{k}", "scalar", 1, 16 * stores, credit=1) for k in B2]
        keyed = Signal(ph, "keyed", "vector", 2)
        spread = Signal(ph, "spread", "tensor", U)
        equaled = Signal(ph, "equaled", "vector", U, credit=2)
        summed = Signal(ph, "summed", "tensor", U, credit=U)
        copied = Signal(ph, "copied", "scalar", U, credit=2)
        turns = Signal(ph, "turns", "gpsimd")
        if kind == "sum":
            pairs = [ph.sb(f"pairs{k}", [P, GT, 2], I32) for k in B2]
            pairs_v = self.pairs_d.rearrange("(g p t) c -> g p t c", p=P, t=GT)
        if FV:
            value = [ph.sb(f"value{k}", [P, GT, FV]) for k in B2]
            values_v = values.rearrange("(g p t) c -> g p t c", p=P, t=GT)

        def free(e, it, k):
            summed.wait(e, it, (k + 1) * QUADS - U)

        def load(e):
            with e.Fori(0, IT) as it:
                for k in B2:
                    free(e, it, k)
                    g = bass.ds(it * 2 + k, 1)
                    e.dma_start(rows[k][:, :, :], source[g, :, :, :].rearrange("g p t c -> (g p) t c")).then_inc(loaded[k].sem, 16)
                    if FV:
                        e.dma_start(value[k][:, :, :], values_v[g, :, :, :].rearrange("g p t c -> (g p) t c")).then_inc(loaded[k].sem, 16)
        ph.on("sync", load)

        def pool(e):
            with e.Fori(0, IT) as it:
                for k in B2:
                    loaded[k].wait(e, it, 1)
                    free(e, it, k)
                    e.sem_inc(turns.sem, 1)
                    for t in range(GT):
                        gather(e, got[k][:, t, :], table[:, :], rows[k][:, t, 1:2]).then_inc(gathered[k].sem, 16)
        ph.on("gpsimd", pool)

        def at(q):
            return q // QUADS, slice((q % QUADS) * QT, (q % QUADS + 1) * QT)

        def dve_key(e, it, k):
            loaded[k].wait(e, it, 1)
            free(e, it, k)
            if kind == "sum":
                stored[k].wait(e, it, 0)
                e.tensor_copy(pairs[k][:, :, :], rows[k][:, :, 0:2])
            keyed.mark(e.tensor_copy(key[k][:, :], rows[k][:, :, 0]))

        def pe_spread(e, it, q):
            k, tiles = at(q)
            if q % QUADS == 0:
                keyed.wait(e, it, k + 1)
            equaled.wait(e, it, q - 1)
            for i in range(QT):
                t = tiles.start + i
                last_i = e.transpose(ps_key[q % 2][:, i, :], key[k][:, t:t + 1].to_broadcast([P, P]), self.ident[:, :])
            spread.mark(last_i)

        def dve_equal(e, it, q):
            k, tiles = at(q)
            spread.wait(e, it, q + 1)
            if q % QUADS == 0:
                keyed.wait(e, it, k + 1)
                free(e, it, k)
            equaled.mark(e.tensor_tensor(equal[k][:, tiles, :], ps_key[q % 2][:, :, :], over(key[k][:, tiles], P), ALU.is_equal))

        def pe_sum(e, it, q, ready):
            k, tiles = at(q)
            ready(e, it, q)
            equaled.wait(e, it, q + 1)
            copied.wait(e, it, q - 1)
            for i in range(QT):
                t = tiles.start + i
                last_i = e.matmul(ps_sum[q % 2][:, i, 0:FG], equal[k][:, t, :], got[k][:, t, :], start=True, stop=True)
            summed.mark(last_i)

        def act_copy(e, it, q):
            k, tiles = at(q)
            summed.wait(e, it, q + 1)
            stored[k].wait(e, it, 0)
            copied.mark(e.activation(outs[k][:, tiles, 0:FG], ps_sum[q % 2][:, :, 0:FG], ACT.Copy))
            if q % QUADS == QUADS - 1:
                copied.wait(e, it, q + 1)
                if gat:
                    m_kept.wait(e, it, k + 1)
                g = bass.ds(it * 2 + k, 1)
                e.dma_start(out_v[g, :, :, :].rearrange("g p t c -> (g p) t c"), outs[k][:, :, :]).then_inc(stored[k].sem, 16)
                e.dma_start(last_v[g, :, :], outs[k][P - 1:P, :, :]).then_inc(stored[k].sem, 16)
                if kind == "sum":
                    e.dma_start(pairs_v[g, :, :, :].rearrange("g p t c -> (g p) t c"), pairs[k][:, :, :]).then_inc(stored[k].sem, 16)

        def when_gathered(e, it, q):
            gathered[q // QUADS].wait(e, it, 1)

        if kind == "sum":
            def pe(e):
                with e.Fori(0, IT) as it:
                    for q in range(U + 1):
                        if q < U:
                            pe_spread(e, it, q)
                        if q:
                            pe_sum(e, it, q - 1, when_gathered)

            def dve(e):
                with e.Fori(0, IT) as it:
                    for q in range(U):
                        if q % QUADS == 0:
                            dve_key(e, it, q // QUADS)
                        dve_equal(e, it, q)

            def act(e):
                with e.Fori(0, IT) as it:
                    for q in range(U):
                        act_copy(e, it, q)

        if mlp:
            ps_fill = [ph.ps(f"ps_fill{k}", [P, QT, HF]) for k in B2]
            fills = Signal(ph, "fills", "tensor", U)
            added = Signal(ph, "added", "vector", U, credit=2)
            message = Signal(ph, "message", "scalar", U)

            def pe_fill(e, it, q):
                k, tiles = at(q)
                loaded[k].wait(e, it, 1)
                equaled.wait(e, it, q + 1)
                added.wait(e, it, q - 1)
                for i in range(QT):
                    t = tiles.start + i
                    last_i = e.matmul(ps_fill[q % 2][:, i, :], equal[k][:, t, :], value[k][:, t, :], start=True, stop=True)
                fills.mark(last_i)

            def pe(e):
                with e.Fori(0, IT) as it:
                    for q in range(U + 3):
                        if q < U:
                            pe_spread(e, it, q)
                        if 1 <= q < U + 1:
                            pe_fill(e, it, q - 1)
                        if q >= 3:
                            pe_sum(e, it, q - 3, lambda e, it, q: message.wait(e, it, q + 1))

            def dve(e):
                with e.Fori(0, IT) as it:
                    for q in range(U + 1):
                        if q < U:
                            if q % QUADS == 0:
                                dve_key(e, it, q // QUADS)
                            dve_equal(e, it, q)
                        if q:
                            k, tiles = at(q - 1)
                            fills.wait(e, it, q)
                            gathered[k].wait(e, it, 1)
                            added.mark(e.tensor_tensor(got[k][:, tiles, :], ps_fill[(q - 1) % 2][:, :, :],
                                                       got[k][:, tiles, :], ALU.add))

            def act(e):
                with e.Fori(0, IT) as it:
                    for q in range(U + 2):
                        if q < U:
                            k, tiles = at(q)
                            added.wait(e, it, q + 1)
                            message.mark(e.activation(got[k][:, tiles, :], got[k][:, tiles, :], ACT.Relu))
                        if q >= 2:
                            act_copy(e, it, q - 2)

        if attr:
            w_attr, w_mid, b_rows, one_rows = weights
            ps_at = ph.ps("ps_at", [P, QT, P])
            ps_h = ph.ps("ps_h", [P, QT, P])
            attr_t = [ph.sb(f"attr_t{k}", [DE, QT, P]) for k in B2]
            h_t = [ph.sb(f"h_t{k}", [P, QT, P]) for k in B2]
            attr_up = Signal(ph, "attr_up", "tensor", U)
            attr_down = Signal(ph, "attr_down", "scalar", U)
            first_up = Signal(ph, "first_up", "tensor", U)
            first_down = Signal(ph, "first_down", "vector", U)
            turned = Signal(ph, "turned", "tensor", U)
            relued = Signal(ph, "relued", "scalar", U, credit=1)
            second_up = Signal(ph, "second_up", "tensor", U)
            message = Signal(ph, "message", "scalar", U, credit=1)

            def pe(e):
                with e.Fori(0, IT) as it:
                    for q in range(U + 1):
                        k, tiles = at(min(q, U - 1))
                        if q < U:
                            pe_spread(e, it, q)
                            loaded[k].wait(e, it, 1)
                            relued.wait(e, it, q)
                            for i in range(QT):
                                last_i = e.transpose(ps_at[0:DE, i, :], rows[k][:, tiles.start + i, 2:ROW].bitcast(F32),
                                                     self.ident[:, :])
                            attr_up.mark(last_i)
                            attr_down.wait(e, it, q + 1)
                            message.wait(e, it, q)
                            for i in range(QT):
                                last_i = e.matmul(ps_h[:, i, :], attr_t[q % 2][:, i, :], w_attr[:, :], start=True, stop=True)
                            first_up.mark(last_i)
                        if q:
                            pe_sum(e, it, q - 1, lambda e, it, q: message.wait(e, it, q + 1))
                        if q < U:
                            first_down.wait(e, it, q + 1)
                            for i in range(QT):
                                last_i = e.transpose(ps_at[:, i, :], got[k][:, tiles.start + i, :], self.ident[:, :])
                            turned.mark(last_i)
                            relued.wait(e, it, q + 1)
                            e.matmul(ps_h[:, :, :], one_rows[:, :], b_rows[:, :, :], start=True, stop=True)
                            for i in range(QT):
                                last_i = e.matmul(ps_h[:, i, :], h_t[q % 2][:, i, :], w_mid[:, :], start=False, stop=True,
                                                  skip_group_check=True)
                            second_up.mark(last_i)

            def dve(e):
                with e.Fori(0, IT) as it:
                    for q in range(U):
                        k, tiles = at(q)
                        if q % QUADS == 0:
                            dve_key(e, it, k)
                        dve_equal(e, it, q)
                        first_up.wait(e, it, q + 1)
                        gathered[k].wait(e, it, 1)
                        first_down.mark(e.tensor_tensor(got[k][:, tiles, :], ps_h[:, :, :], got[k][:, tiles, :], ALU.add))

            def act(e):
                with e.Fori(0, IT) as it:
                    for q in range(U + 1):
                        k, tiles = at(min(q, U - 1))
                        if q < U:
                            attr_up.wait(e, it, q + 1)
                            attr_down.mark(e.activation(attr_t[q % 2][:, :, :], ps_at[0:DE, :, :], ACT.Copy))
                        if q:
                            act_copy(e, it, q - 1)
                        if q < U:
                            turned.wait(e, it, q + 1)
                            relued.mark(e.activation(h_t[q % 2][:, :, :], ps_at[:, :, :], ACT.Relu))
                            second_up.wait(e, it, q + 1)
                            message.mark(e.activation(got[k][:, tiles, :], ps_h[:, :, :], ACT.Relu))

        if gat:
            W = GT * heads
            key_rep = [ph.sb(f"key_rep{k}", [P, GT, heads]) for k in B2]
            key_t = ph.sb("key_t", [P, P])
            mask = ph.sb("mask", [P, P + 1])
            score = ph.sb("score", [P, GT, heads])
            run = ph.sb("run", [P, P])
            top = ph.sb("top", [P, P])
            diff = ph.sb("diff", [P, GT, heads])
            small = ph.ps("small", [P, 4, P])
            repeated = Signal(ph, "repeated", "vector", 2)
            key_up = Signal(ph, "key_up", "tensor", 2)
            key_down = Signal(ph, "key_down", "scalar", 2)
            filled = Signal(ph, "filled", "tensor", 2)
            scores = Signal(ph, "scores", "vector", 12)
            score_up = Signal(ph, "score_up", "tensor", 2)
            topped = Signal(ph, "topped", "vector", 2)
            top_up = Signal(ph, "top_up", "tensor", 2)
            less = Signal(ph, "less", "vector", 2)
            exped = Signal(ph, "exped", "scalar", 2)
            m_kept = Signal(ph, "m_kept", "scalar", 2, credit=1)
            message = Signal(ph, "message", "vector", 2, credit=1)
            edges = Signal(ph, "edges", "vector")

            def pe(e):
                with e.Fori(0, IT) as it:
                    for k in B2:
                        for q in range(k * QUADS, (k + 1) * QUADS):
                            pe_spread(e, it, q)
                        repeated.wait(e, it, k + 1)
                        message.wait(e, it, k)
                        m_kept.wait(e, it, k)
                        key_up.mark(e.transpose(small[0:W, 0, :], key_rep[k][:, :, :].rearrange("p t h -> p (t h)"), self.ident[:, :]))
                        loaded[k].wait(e, it, 1)
                        equaled.wait(e, it, (k + 1) * QUADS)
                        key_down.wait(e, it, k + 1)
                        for t in range(GT):
                            last_i = e.matmul(small[:, 1, t * heads:(t + 1) * heads], equal[k][:, t, :], value[k][:, t, 0:heads],
                                              start=True, stop=True)
                        filled.mark(last_i)
                        scores.wait(e, it, 6 * k + 4)
                        score_up.mark(e.transpose(small[0:W, 2, :], score[:, :, :].rearrange("p t h -> p (t h)"), self.ident[:, :]))
                        topped.wait(e, it, k + 1)
                        top_up.mark(e.transpose(small[:, 3, :], top[:, :], self.ident[:, :]))
                        for q in range(k * QUADS, (k + 1) * QUADS):
                            pe_sum(e, it, q, lambda e, it, q: message.wait(e, it, q // QUADS + 1))

            def dve(e):
                edges.mark(e.memset(mask[:, :], -BIG))
                edges.mark(e.memset(top[:, :], 0.0))
                edges.wait(e, 0, 2)
                with e.Fori(0, IT) as it:
                    for k in B2:
                        n = [6 * k]

                        def do(i):
                            scores.mark(i)
                            n[0] += 1
                            scores.wait(e, it, n[0])
                        dve_key(e, it, k)
                        keyed.wait(e, it, k + 1)
                        repeated.mark(e.tensor_copy(key_rep[k][:, :, :], over(key[k][:, :], heads)))
                        for q in range(k * QUADS, (k + 1) * QUADS):
                            dve_equal(e, it, q)
                        key_down.wait(e, it, k + 1)
                        message.wait(e, it, k)
                        do(e.tensor_tensor(mask[0:W, 1:P], key_t[0:W, 1:P], key_t[0:W, 0:P - 1], ALU.is_equal))
                        do(e.tensor_scalar(mask[0:W, 1:P], mask[0:W, 1:P], -1.0, BIG, ALU.add, ALU.mult))
                        filled.wait(e, it, k + 1)
                        gathered[k].wait(e, it, 1)
                        do(e.tensor_tensor(diff[:, :, :], small[:, 1, 0:W].rearrange("p (t h) -> p t h", h=heads),
                                           got[k][:, :, HF:FG], ALU.add))
                        do(e.scalar_tensor_tensor(score[:, :, :], diff[:, :, :], 0.2, diff[:, :, :], ALU.mult, ALU.max))
                        score_up.wait(e, it, k + 1)
                        do(e.tensor_tensor_scan(run[0:W, :], mask[0:W, 0:P], small[0:W, 2, :], 0.0, ALU.add, ALU.max))
                        topped.mark(e.tensor_tensor_scan(top[0:W, ::-1], mask[0:W, P:0:-1], run[0:W, ::-1], 0.0, ALU.add, ALU.max))
                        top_up.wait(e, it, k + 1)
                        less.mark(e.tensor_tensor(diff[:, :, :], score[:, :, :],
                                                  small[:, 3, 0:W].rearrange("p (t h) -> p t h", h=heads), ALU.subtract))
                        exped.wait(e, it, k + 1)
                        do(e.tensor_copy(diff[:, :, :], got[k][:, :, HF:FG]))
                        hs = got[k][:, :, 0:HF].rearrange("p t (h c) -> p t h c", h=heads)
                        message.mark(e.tensor_tensor(hs, hs, over(diff[:, :, :], ch), ALU.mult))

            def act(e):
                with e.Fori(0, IT) as it:
                    for k in B2:
                        key_up.wait(e, it, k + 1)
                        message.wait(e, it, k)
                        key_down.mark(e.activation(key_t[0:W, :], small[0:W, 0, :], ACT.Copy))
                        less.wait(e, it, k + 1)
                        exped.mark(e.activation(got[k][:, :, HF:FG], diff[:, :, :], ACT.Exp))
                        stored[k].wait(e, it, 0)
                        m_kept.mark(e.activation(outs[k][:, :, FG:FO], small[:, 3, 0:W].rearrange("p (t h) -> p t h", h=heads), ACT.Copy))
                        for q in range(k * QUADS, (k + 1) * QUADS):
                            act_copy(e, it, q)

        ph.on("tensor", pe)
        ph.on("vector", dve)
        ph.on("scalar", act)
        ph.on("scalar", lambda e: [stored[k].wait(e, 0, IT) for k in B2])
        ph.run()

    def linear(self, ph, name, src, weight, cols, evacuate, steps, after=None):
        K, B, R = src.shape[2], 2, range(2)
        ps_t = [ph.ps(f"{name}_ps_t{k}", [P, B, P]) for k in R]
        src_t = [ph.sb(f"{name}_src_t{k}", [P, B, P]) for k in R]
        ps_o = [ph.ps(f"{name}_ps_o{k}", [P, B, cols]) for k in R]
        turned = Signal(ph, f"{name}_turned", "tensor")
        kept = Signal(ph, f"{name}_kept", "scalar")
        made = Signal(ph, f"{name}_made", "tensor")
        out = Signal(ph, f"{name}_out", "vector")
        batches = NT // B
        before = after.now if after else None

        def pe(e):
            def turn(b):
                if b >= 2:
                    kept.wait(e, 0, b - 1)
                for i in range(B):
                    last = e.transpose(ps_t[b % 2][0:K, i, :], src[:, b * B + i, :], self.ident[:, :])
                turned.mark(last)
            if before:
                e.wait_ge(*before)
            turn(0)
            for b in range(batches):
                if b + 1 < batches:
                    turn(b + 1)
                kept.wait(e, 0, b + 1)
                if b >= 2:
                    out.wait(e, 0, (b - 1) * steps)
                for i in range(B):
                    last = e.matmul(ps_o[b % 2][:, i, :], src_t[b % 2][0:K, i, :], weight, start=True, stop=True)
                made.mark(last)

        def act(e):
            for b in range(batches):
                turned.wait(e, 0, b + 1)
                if b >= 2:
                    made.wait(e, 0, b - 1)
                kept.mark(e.activation(src_t[b % 2][0:K, :, :], ps_t[b % 2][0:K, :, :], ACT.Copy))

        def dve(e):
            if before:
                e.wait_ge(*before)
            for b in range(batches):
                made.wait(e, 0, b + 1)
                makers = evacuate(e, b * B, ps_o[b % 2])
                assert len(makers) == steps
                for n, make in enumerate(makers):
                    if b + n:
                        out.wait(e, 0, b * steps + n)
                    out.mark(make())
        ph.on("tensor", pe)
        ph.on("scalar", act)
        ph.on("vector", dve)
        ph.on("vector", lambda e: out.wait(e, 0, batches * steps))
        return lambda e: out.wait(e, 0, batches * steps)

    def layernorm(self, ph, c):
        x, h = self.x, self.feat[:, :, 0:D]
        mean = ph.sb("mean", [P, NT])
        var = ph.sb("var", [P, NT])
        root = ph.sb("root", [P, NT])
        inv = ph.sb("inv", [P, NT])
        err = ph.sb("err", [P, NT])
        cen = self.feat[:, :, D:2 * D]
        c.v(lambda e: e.reduce_sum(mean[:, :], x[:, :, :], axis=AX.X))
        c.v(lambda e: e.tensor_scalar(mean[:, :], mean[:, :], 1.0 / D, None, ALU.mult))
        c.v(lambda e: e.tensor_tensor(cen, x[:, :, :], over(mean[:, :], D), ALU.subtract))
        c.v(lambda e: e.tensor_tensor(h, cen, cen, ALU.mult))
        c.v(lambda e: e.reduce_sum(var[:, :], h, axis=AX.X))
        c.v(lambda e: e.tensor_scalar(var[:, :], var[:, :], 1.0 / D, EPS, ALU.mult, ALU.add))
        c.a(lambda e: e.activation(root[:, :], var[:, :], ACT.Sqrt))
        self.inverse_root(c, inv[:, :], root[:, :], var[:, :], err[:, :])
        c.v(lambda e: e.tensor_tensor(h, cen, over(inv[:, :], D), ALU.mult))
        c.v(lambda e: e.tensor_scalar(h, h, 0.0, None, ALU.max))

    def inverse_root(self, c, inv, root, square, err):
        c.v(lambda e: e.reciprocal(inv, root))
        c.v(lambda e: e.tensor_tensor(err, inv, inv, ALU.mult))
        c.v(lambda e: e.tensor_tensor(err, err, square, ALU.mult))
        c.v(lambda e: e.tensor_scalar(err, err, -0.5, 1.5, ALU.mult, ALU.add))
        c.v(lambda e: e.tensor_tensor(inv, inv, err, ALU.mult))

    def broadcast_row(self, row, n):
        return row.rearrange("(a n) -> a n", a=1).to_broadcast([P, n])

    def nodes_out(self, table):
        return table.rearrange("(p t) c -> p t c", t=NT)

    def finish_sums(self, name, s, out, last, FO, heads=0, feat=None):
        HF = FO - 2 * heads
        ph = Phase(self.nc, name)
        c = Chain(ph)
        rows = ph.sb("rows", [P, TB, FO])
        patch = ph.sb("patch", [P, TB, FO])
        acc_t = ph.sb("acc_t", [P, T])
        run = ph.sb("run", [P, T + 1])
        ps = [ph.ps(f"ps{k}", [P, QT, P]) for k in range(2)]
        link = self.links[:, s, :]
        c.load(lambda e: e.dma_start(rows[:, :, :], last.rearrange("(b q) c -> q b c", q=P)))
        c.g(lambda e: e.memset(patch[:, :, :], 0.0))
        c.indirect(lambda e: [gather(e, patch[:, b, :], out[:, :], self.patch_row[:, s, b:b + 1], EP - 1) for b in range(TB)], TB)

        def transposed(to, cols, n):
            def quad(b0):
                m = min(QT, TB - b0)
                c.step("tensor", lambda e: [e.transpose(ps[0][0:n, i, :], rows[:, b0 + i, cols], self.ident[:, :]) for i in range(m)], m)
                c.a(lambda e: e.activation(to[0:n, b0 * P:(b0 + m) * P], ps[0][0:n, 0:m, :].rearrange("p a b -> p (a b)"), ACT.Copy))
            for b0 in range(0, TB, QT):
                quad(b0)

        def back(to, of, n):
            def quad(b0):
                m = min(QT, TB - b0)
                c.step("tensor", lambda e: [e.transpose(ps[1][:, i, 0:n], of[0:n, (b0 + i) * P:(b0 + i + 1) * P], self.ident[0:n, 0:n]) for i in range(m)], m)
                c.a(lambda e: e.activation(to[:, b0:b0 + m, :], ps[1][:, 0:m, 0:n], ACT.Copy))
            for b0 in range(0, TB, QT):
                quad(b0)
        if not heads:
            transposed(acc_t, slice(0, FO), FO)
            c.v(lambda e: e.memset(run[:, 0:1], 0.0))
            c.v(lambda e: e.tensor_tensor_scan(run[0:FO, 1:T + 1], link[0:FO, :], acc_t[0:FO, :], 0.0, ALU.mult, ALU.add))
            back(rows, run, FO)
            c.v(lambda e: e.tensor_tensor(patch[:, :, :], patch[:, :, :], rows[:, :, :], ALU.add))
        else:
            m_t = ph.sb("m_t", [heads, T])
            s_t = ph.sb("s_t", [heads, T])
            m_run = ph.sb("m_run", [heads, T + 1])
            s_run = ph.sb("s_run", [heads, T + 1])
            scale = ph.sb("scale", [heads, T])
            decay = ph.sb("decay", [heads, T])
            neg = ph.sb("neg", [heads, T])
            decay_f = ph.sb("decay_f", [P, T])
            pick = ph.sb("pick", [heads, HF])
            ch = HF // heads
            c.g(lambda e: e.memset(pick[:, :], 1.0))
            c.g(lambda e: e.affine_select(out=pick[:, :], in_=pick[:, :], compare_op=ALU.is_ge, fill=0.0, base=0,
                                          pattern=[[1, HF]], channel_multiplier=-ch))
            c.g(lambda e: e.affine_select(out=pick[:, :], in_=pick[:, :], compare_op=ALU.is_ge, fill=0.0, base=ch - 1,
                                          pattern=[[-1, HF]], channel_multiplier=ch))
            transposed(m_t, slice(HF + heads, FO), heads)
            transposed(s_t, slice(HF, HF + heads), heads)
            transposed(acc_t, slice(0, HF), HF)
            H = slice(0, heads)
            c.v(lambda e: [e.memset(m_run[:, 0:1], -BIG), e.memset(s_run[:, 0:1], 0.0), e.memset(run[:, 0:1], 0.0),
                           e.tensor_scalar(neg[:, :], link[H, :], -1.0, BIG, ALU.add, ALU.mult)], 4)
            c.v(lambda e: e.tensor_tensor_scan(m_run[:, 1:T + 1], neg[:, :], m_t[:, :], 0.0, ALU.add, ALU.max))
            c.v(lambda e: [e.tensor_tensor(scale[:, :], m_t[:, :], m_run[:, 1:T + 1], ALU.subtract),
                           e.tensor_tensor(decay[:, :], m_run[:, 0:T], m_run[:, 1:T + 1], ALU.subtract)], 2)
            c.v(lambda e: e.tensor_scalar(decay[:, :], decay[:, :], 0.0, None, ALU.min))
            c.a(lambda e: [e.activation(scale[:, :], scale[:, :], ACT.Exp), e.activation(decay[:, :], decay[:, :], ACT.Exp)], 2)
            c.v(lambda e: [e.tensor_tensor(decay[:, :], decay[:, :], link[H, :], ALU.mult),
                           e.tensor_tensor(s_t[:, :], s_t[:, :], scale[:, :], ALU.mult)], 2)
            c.v(lambda e: e.tensor_tensor_scan(s_run[:, 1:T + 1], decay[:, :], s_t[:, :], 0.0, ALU.mult, ALU.add))

            def scaled(t0):
                w = min(512, T - t0)
                flat = [p[:, :, :].rearrange("p a b -> p (a b)") for p in ps]
                c.step("tensor", lambda e: [e.matmul(flat[k][0:HF, 0:w], pick[:, :], of[:, t0:t0 + w], start=True, stop=True)
                                            for k, of in enumerate((scale, decay))], 2)
                c.v(lambda e: [e.tensor_tensor(acc_t[0:HF, t0:t0 + w], acc_t[0:HF, t0:t0 + w], flat[0][0:HF, 0:w], ALU.mult),
                               e.tensor_copy(decay_f[0:HF, t0:t0 + w], flat[1][0:HF, 0:w])], 2)
            for t0 in range(0, T, 512):
                scaled(t0)
            c.v(lambda e: e.tensor_tensor_scan(run[0:HF, 1:T + 1], decay_f[0:HF, :], acc_t[0:HF, :], 0.0, ALU.mult, ALU.add))
            back(rows[:, :, 0:HF], run, HF)
            back(rows[:, :, HF:HF + heads], s_run, heads)
            back(rows[:, :, HF + heads:FO], m_run, heads)
            self.merge(ph, c, patch[:, :, :], rows[:, :, 0:HF], rows[:, :, HF:HF + heads], rows[:, :, HF + heads:FO],
                       TB, heads, ch)
        c.indirect(lambda e: [scatter(e, out[:, :], self.patch_row[:, s, b:b + 1], patch[:, b, :], EP - 1) for b in range(TB)], TB)
        c.finish("gpsimd")
        ph.run()

    def merge_buffers(self, ph, n, heads, ch):
        return [ph.sb(f"mg_m", [P, n, heads]), ph.sb("mg_a", [P, n, heads]), ph.sb("mg_b", [P, n, heads]),
                ph.sb("mg_s", [P, n, heads]), ph.sb("mg_f", [P, n, heads * ch])]

    def merge(self, ph, c, to, acc, s, m, n, heads, ch, bufs=None):
        HF = heads * ch
        top, ea, eb, sb, f = bufs or self.merge_buffers(ph, n, heads, ch)
        to_acc, to_s, to_m = to[:, :, 0:HF], to[:, :, HF:HF + heads], to[:, :, HF + heads:HF + 2 * heads]

        def by_head(a):
            return a.rearrange("p t (h c) -> p t h c", h=heads)
        c.v(lambda e: e.tensor_tensor(top[:, :, :], to_m, m, ALU.max))
        c.v(lambda e: [e.tensor_tensor(ea[:, :, :], to_m, top[:, :, :], ALU.subtract),
                       e.tensor_tensor(eb[:, :, :], m, top[:, :, :], ALU.subtract)], 2)
        c.a(lambda e: [e.activation(ea[:, :, :], ea[:, :, :], ACT.Exp), e.activation(eb[:, :, :], eb[:, :, :], ACT.Exp)], 2)
        one = s is None
        c.v(lambda e: [e.tensor_tensor(by_head(to_acc), by_head(to_acc), over(ea[:, :, :], ch), ALU.mult),
                       e.tensor_tensor(by_head(f[:, :, :]), by_head(acc), over(eb[:, :, :], ch), ALU.mult),
                       e.tensor_tensor(to_s, to_s, ea[:, :, :], ALU.mult),
                       e.tensor_copy(sb[:, :, :], eb[:, :, :]) if one else
                       e.tensor_tensor(sb[:, :, :], s, eb[:, :, :], ALU.mult),
                       e.tensor_copy(to_m, top[:, :, :])], 5)
        c.v(lambda e: [e.tensor_tensor(to_acc, to_acc, f[:, :, :], ALU.add), e.tensor_tensor(to_s, to_s, sb[:, :, :], ALU.add)], 2)

    def collect(self, c, to, s, out):
        c.indirect(lambda e: [gather(e, to[:, t, :], out[:, :], self.end_row[:, s, t:t + 1], EP - 1) for t in range(NT)], NT)

    def spread_values(self, ph, c, s, rows, table, values):
        F = values.shape[1]
        of_tile = ph.sb("of_tile", [P, TB, F])
        c.indirect(lambda e: [gather(e, of_tile[:, b, :], table[:, :], self.first_key[:, s, b:b + 1]) for b in range(TB)], TB)
        c.indirect(lambda e: [scatter(e, values[:, :], self.first_row[:, b:b + 1], of_tile[:, b, :]) for b in range(TB)]
                   + [scatter(e, values[:, :], self.start_row[:, s, t:t + 1], rows[:, t, :], EP - 1) for t in range(NT)], TB + NT)

    def block0(self):
        ins = self.ins
        self.table0 = self.dram("table0", (NP, D))
        ph = Phase(self.nc, "b0a")
        c = Chain(ph)
        self.layernorm(ph, c)
        wh = ph.sb("wh", [D, H0, D])
        c.load(lambda e: e.dma_start(wh[:, :, :], ins["L0_gnn_Wh"].rearrange("h d e -> d h e")))
        h = self.feat[:, :, 0:D]
        prod = [ph.sb(f"prod{k}", [P, 2, H0, D]) for k in range(2)]
        score = self.score0 = self.feat[:, :, D:D + H0]

        def evac(e, t, ps):
            pr = prod[t // 2 % 2]
            hb = h[:, t:t + 2, :].unsqueeze(2).to_broadcast([P, 2, H0, D])
            return [lambda: e.tensor_tensor(pr[:, :, :, :], ps[:, :, :].rearrange("p t (h e) -> p t h e", h=H0), hb, ALU.mult),
                    lambda: e.reduce_sum(score[:, t:t + 2, :], pr[:, :, :, :], axis=AX.X)]
        self.linear(ph, "lin", h, wh[:, :, :].rearrange("d h e -> d (h e)"), H0 * D, evac, 2, after=c)
        ph.run()

        ph = Phase(self.nc, "b0b")
        c = Chain(ph)
        top = ph.sb("top", [P, H0])
        top_all = ph.sb("top_all", [P, H0])
        total = ph.sb("total", [P, H0])
        total_all = ph.sb("total_all", [P, H0])
        att = ph.sb("att", [P, NT, H0])
        c.g(lambda e: e.affine_select(out=att[:, :, :], in_=score, compare_op=ALU.is_gt, fill=-BIG, base=N,
                                      pattern=[[-1, NT], [0, H0]], channel_multiplier=-NT))
        c.v(lambda e: e.tensor_reduce(top[:, :], att[:, :, :].rearrange("p t h -> p h t"), AX.X, ALU.max))
        c.g(lambda e: e.partition_all_reduce(top_all[:, :], top[:, :], P, RMAX))
        c.v(lambda e: e.tensor_tensor(att[:, :, :], att[:, :, :], top_all[:, :].unsqueeze(1).to_broadcast([P, NT, H0]), ALU.subtract))
        c.a(lambda e: e.activation(att[:, :, :], att[:, :, :], ACT.Exp, scale=float(D) ** -0.5))
        c.v(lambda e: e.reduce_sum(total[:, :], att[:, :, :].rearrange("p t h -> p h t"), axis=AX.X))
        c.g(lambda e: e.partition_all_reduce(total_all[:, :], total[:, :], P, RADD))
        c.v(lambda e: e.reciprocal(total_all[:, :], total_all[:, :]))
        c.v(lambda e: e.tensor_tensor(att[:, :, :], att[:, :, :], total_all[:, :].unsqueeze(1).to_broadcast([P, NT, H0]), ALU.mult))
        wo = ph.sb("wo", [D, H0, D])
        c.load(lambda e: e.dma_start(wo[:, :, :], ins["L0_gnn_weight"].rearrange("(h d) e -> d h e", h=H0)))
        prod = [ph.sb(f"prod{k}", [P, 2, H0, D]) for k in range(2)]
        y = self.feat[:, :, D:2 * D]

        def evac(e, t, ps):
            pr = prod[t // 2 % 2]
            return [lambda: e.tensor_tensor(pr[:, :, :, :], ps[:, :, :].rearrange("p t (h e) -> p t h e", h=H0),
                                            over(att[:, t:t + 2, :], D), ALU.mult),
                    lambda: e.reduce_sum(y[:, t:t + 2, :], pr[:, :, :, :].rearrange("p t h e -> p t e h"), axis=AX.X)]
        wait = self.linear(ph, "lin", h, wo[:, :, :].rearrange("d h e -> d (h e)"), H0 * D, evac, 2, after=c)
        ph.on("sync", wait)
        c.load(lambda e: e.dma_start(self.nodes_out(self.table0), y))
        c.finish()
        ph.run()
        out = self.dram("out0", (EP, D))
        last = self.dram("last0", (T, D))
        self.edge_pass("e0", "sum", 0, self.table0, out, last)
        self.finish_sums("f0", 0, out, last, D)
        ph = Phase(self.nc, "b0c")
        c = Chain(ph)
        agg, ex = ph.sb("agg", [P, NT, D]), ph.sb("ex", [P, NT, D])
        c.g(lambda e: e.memset(agg[:, :, :], 0.0))
        self.collect(c, agg, 0, out)
        self.elu(c, agg[:, :, :], ex[:, :, :])
        c.v(lambda e: e.tensor_tensor(self.x[:, :, :], self.x[:, :, :], agg[:, :, :], ALU.add))
        c.finish()
        ph.run()

    def elu(self, c, a, tmp):
        c.v(lambda e: e.tensor_scalar(tmp, a, 0.0, None, ALU.min))
        c.a(lambda e: e.activation(tmp, tmp, ACT.Exp))
        c.v(lambda e: e.tensor_scalar(tmp, tmp, -1.0, None, ALU.add))
        c.v(lambda e: e.scalar_tensor_tensor(a, a, 0.0, tmp, ALU.max, ALU.add))

    def block1(self):
        ins = self.ins
        table_q, table_p = self.dram("table_q", (NP, D)), self.dram("table_p", (NP, D))
        values = self.dram("values1", (EP, D))
        self.zero_values("z1", values)
        ph = Phase(self.nc, "b1a")
        c = Chain(ph)
        self.layernorm(ph, c)
        w = ph.sb("w", [D, 2, D])
        bias = ph.sb("bias", [P, D])
        self.own1 = self.feat[:, :, 0:D]
        c.load(lambda e: [e.dma_start(w[:, a, :], ins["L1_gnn_W"][:, a * D:(a + 1) * D].rearrange("o i -> i o")) for a in range(2)]
               + [e.dma_start(bias[:, :], self.broadcast_row(ins["L1_gnn_b"], D))], 3)
        h = self.feat[:, :, 0:D]
        both = ph.sb("both", [P, NT, 2 * D])

        def evac(e, t, ps):
            return [lambda: e.tensor_tensor(both[:, t:t + 2, 0:D], ps[:, :, 0:D], bias[:, :].unsqueeze(1).to_broadcast([P, 2, D]), ALU.add),
                    lambda: e.tensor_copy(both[:, t:t + 2, D:2 * D], ps[:, :, D:2 * D])]
        wait = self.linear(ph, "lin", h, w[:, :, :].rearrange("i a o -> i (a o)"), 2 * D, evac, 2, after=c)
        ph.on("sync", wait)
        c.load(lambda e: [e.dma_start(self.nodes_out(table_p), both[:, :, 0:D]), e.dma_start(self.nodes_out(table_q), both[:, :, D:2 * D])], 2)
        self.spread_values(ph, c, 1, both[:, :, 0:D], table_p, values)
        c.finish("gpsimd")
        ph.run()
        out, last = self.dram("out1", (EP, D)), self.dram("last1", (T, D))
        self.edge_pass("e1", "mlp", 1, table_q, out, last, values=values)
        self.finish_sums("f1", 1, out, last, D)
        ph = Phase(self.nc, "b1c")
        c = Chain(ph)
        agg = self.feat[:, :, 0:D]
        own = self.feat[:, :, D:2 * D]
        w = ph.sb("w", [D, D])
        c.g(lambda e: e.memset(agg, 0.0))
        self.collect(c, agg, 1, out)
        c.load(lambda e: [e.dma_start(w[:, :], ins["L1_gnn_W"][:, D:2 * D].rearrange("o i -> i o")),
                          e.dma_start(own, self.nodes_out(table_p))], 2)

        def evac(e, t, ps):
            o, x = own[:, t:t + 2, :], self.x[:, t:t + 2, :]
            return [lambda: e.tensor_tensor(o, ps[:, :, :], o, ALU.add),
                    lambda: e.scalar_tensor_tensor(x, o, 0.0, x, ALU.max, ALU.add)]
        self.linear(ph, "lin", agg, w[:, :], D, evac, 2, after=c)
        ph.run()

    def zero_values(self, name, values):
        F = values.shape[1]
        ph = Phase(self.nc, name)
        c = Chain(ph)
        part = EP // P // 16
        zeros = ph.sb("zeros", [P, part * F])
        v = values.rearrange("(n p r) c -> n p (r c)", p=P, r=part)
        c.v(lambda e: e.memset(zeros[:, :], 0.0))
        c.load(lambda e: [e.dma_start(v[n, :, :], zeros[:, :]) for n in range(16)], 16)
        c.finish()
        ph.run()

    def gat_layer(self, n, heads, ch, K, src_cols):
        ins = self.ins
        HF = heads * ch
        FG, FO = HF + heads, HF + 2 * heads
        table, own = self.dram(f"gat_table{n}", (NP, FG)), self.dram(f"gat_dst{n}", (NP, HEADS))
        ph = Phase(self.nc, f"g{n}a")
        c = Chain(ph)
        if n == 1:
            self.layernorm(ph, c)
        w = ph.sb("w", [K, HF])
        a_src, a_dst = ph.sb("a_src", [P, HF]), ph.sb("a_dst", [P, HF])
        hid = ph.sb("hid", [P, NT, FG])
        dst = ph.sb("dst", [P, NT, HEADS])
        tmp = [ph.sb(f"tmp{k}", [P, 2, HF]) for k in range(2)]
        c.load(lambda e: [e.dma_start(w[:, :], ins[f"L2_gnn_W{n}"]),
                          e.dma_start(a_src[:, :], self.broadcast_row(ins[f"L2_gnn_as{n}"].rearrange("h c -> (h c)"), HF)),
                          e.dma_start(a_dst[:, :], self.broadcast_row(ins[f"L2_gnn_ad{n}"].rearrange("h c -> (h c)"), HF))], 3)
        c.g(lambda e: e.memset(dst[:, :, :], 0.0))

        def evac(e, t, ps):
            hh = hid[:, t:t + 2, 0:HF]

            def wide(a):
                return a[:, :].unsqueeze(1).to_broadcast([P, 2, HF])

            def by_head(a):
                return a[:, :, :].rearrange("p t (h c) -> p t h c", h=heads)
            return [lambda: e.tensor_copy(hh, ps[:, :, :]),
                    lambda: e.tensor_tensor(tmp[0][:, :, :], hh, wide(a_src), ALU.mult),
                    lambda: e.reduce_sum(hid[:, t:t + 2, HF:FG], by_head(tmp[0]), axis=AX.X),
                    lambda: e.tensor_tensor(tmp[1][:, :, :], hh, wide(a_dst), ALU.mult),
                    lambda: e.reduce_sum(dst[:, t:t + 2, 0:heads], by_head(tmp[1]), axis=AX.X)]
        wait = self.linear(ph, "lin", self.feat[:, :, 0:K], w[:, :], HF, evac, 5, after=c)
        ph.on("sync", wait)
        c.load(lambda e: [e.dma_start(self.nodes_out(table), hid[:, :, :]), e.dma_start(self.nodes_out(own), dst[:, :, :])], 2)
        self.spread_values(ph, c, 0, dst, own, self.values2)
        c.finish("gpsimd")
        ph.run()
        out, last = self.dram(f"gat_out{n}", (EP, FO)), self.dram(f"gat_last{n}", (T, FO))
        self.edge_pass(f"eg{n}", "gat", 0, table, out, last, values=self.values2, heads=heads, ch=ch)
        self.finish_sums(f"fg{n}", 0, out, last, FO, heads)

        ph = Phase(self.nc, f"g{n}c")
        c = Chain(ph)
        part = NT // 7
        agg = ph.sb("agg", [P, NT, FO])
        hid = ph.sb("hid", [P, part, FG])
        dst = ph.sb("dst", [P, NT, HEADS])
        e_own = ph.sb("e_own", [P, part, heads])
        bias = ph.sb("bias", [P, HF])
        inv = ph.sb("inv", [P, part, heads])
        bufs = self.merge_buffers(ph, part, heads, ch)
        c.g(lambda e: [e.memset(agg[:, :, 0:FG], 0.0), e.memset(agg[:, :, FG:FO], -BIG)], 2)
        self.collect(c, agg, 0, out)
        c.load(lambda e: [e.dma_start(dst[:, :, :], self.nodes_out(own)), e.dma_start(bias[:, :], self.broadcast_row(ins[f"L2_gnn_b{n}"], HF))], 2)

        def columns(t0):
            ts = slice(t0, t0 + part)
            c.load(lambda e: e.dma_start(hid[:, :, :], self.nodes_out(table)[:, ts, :]))
            c.v(lambda e: e.tensor_tensor(e_own[:, :, :], hid[:, :, HF:FG], dst[:, ts, 0:heads], ALU.add))
            c.v(lambda e: e.scalar_tensor_tensor(e_own[:, :, :], e_own[:, :, :], 0.2, e_own[:, :, :], ALU.mult, ALU.max))
            self.merge(ph, c, agg[:, ts, :], hid[:, :, 0:HF], None, e_own[:, :, :], part, heads, ch, bufs)
            c.v(lambda e: e.tensor_scalar(inv[:, :, :], agg[:, ts, HF:FG], 1e-16, None, ALU.add))
            c.v(lambda e: e.reciprocal(inv[:, :, :], inv[:, :, :]))

            def by_head(a):
                return a.rearrange("p t (h c) -> p t h c", h=heads)
            c.v(lambda e: e.tensor_tensor(by_head(self.feat[:, ts, 0:HF]), by_head(agg[:, ts, 0:HF]), over(inv[:, :, :], ch), ALU.mult))
            c.v(lambda e: e.tensor_tensor(self.feat[:, ts, 0:HF], self.feat[:, ts, 0:HF],
                                          bias[:, :].unsqueeze(1).to_broadcast([P, part, HF]), ALU.add))
            if n < 3:
                self.elu(c, self.feat[:, ts, 0:HF], bufs[4][:, :, :])
        for t0 in range(0, NT, part):
            columns(t0)
        c.finish()
        ph.run()

    def block2(self):
        self.values2 = self.dram("values2", (EP, HEADS))
        self.zero_values("z2", self.values2)
        HID = HEADS * CH
        self.gat_layer(1, HEADS, CH, D, None)
        self.gat_layer(2, HEADS, CH, HID, None)
        self.gat_layer(3, 1, D, HID, None)
        ph = Phase(self.nc, "b2d")
        c = Chain(ph)
        w, bias = ph.sb("w", [D, D]), ph.sb("bias", [P, D])
        c.load(lambda e: [e.dma_start(w[:, :], self.ins["L2_gnn_Wp"]), e.dma_start(bias[:, :], self.broadcast_row(self.ins["L2_gnn_bp"], D))], 2)
        y = self.feat[:, :, D:2 * D]
        self.linear(ph, "lin", self.feat[:, :, 0:D], w[:, :], D, lambda e, t, ps: [
            lambda: e.tensor_tensor(y[:, t:t + 2, :], ps[:, :, :], bias[:, :].unsqueeze(1).to_broadcast([P, 2, D]), ALU.add)], 1, after=c)
        ph.run()
        ph = Phase(self.nc, "b2e")
        c = Chain(ph)
        sq = ph.sb("sq", [P, NT, D])
        norm = ph.sb("norm", [P, NT])
        c.v(lambda e: e.tensor_tensor(sq[:, :, :], y, y, ALU.mult))
        c.v(lambda e: e.reduce_sum(norm[:, :], sq[:, :, :], axis=AX.X))
        root, inv, err = (ph.sb(k, [P, NT]) for k in ("root", "inv", "err"))
        c.v(lambda e: e.tensor_scalar(norm[:, :], norm[:, :], 1e-24, None, ALU.max))
        c.a(lambda e: e.activation(root[:, :], norm[:, :], ACT.Sqrt))
        self.inverse_root(c, inv[:, :], root[:, :], norm[:, :], err[:, :])
        c.v(lambda e: e.tensor_tensor(y, y, over(inv[:, :], D), ALU.mult))
        c.v(lambda e: e.tensor_tensor(self.x[:, :, :], self.x[:, :, :], y, ALU.add))
        ph.run()

    def block3(self):
        ins = self.ins
        H = 2 * D
        table = self.dram("table3", (NP, H))
        ph = Phase(self.nc, "b3a")
        c = Chain(ph)
        self.layernorm(ph, c)
        w, bias = ph.sb("w", [D, H]), ph.sb("bias", [P, H])
        hid = ph.sb("hid", [P, NT, H])
        c.load(lambda e: [e.dma_start(w[:, :], ins["L3_gnn_W1a"][0:D, :]), e.dma_start(bias[:, :], self.broadcast_row(ins["L3_gnn_b1a"], H))], 2)
        wait = self.linear(ph, "lin", self.feat[:, :, 0:D], w[:, :], H, lambda e, t, ps: [
            lambda: e.tensor_tensor(hid[:, t:t + 2, :], ps[:, :, :], bias[:, :].unsqueeze(1).to_broadcast([P, 2, H]), ALU.add)], 1, after=c)
        ph.on("sync", wait)
        c.load(lambda e: e.dma_start(self.nodes_out(table), hid[:, :, :]))
        c.finish()
        ph.run()

        top = Phase(self.nc, "w3")
        w_attr = top.sb("w_attr", [DE, H])
        w_mid = top.sb("w_mid", [H, H])
        b_rows = top.sb("b_rows", [3, QT, H], BF16)
        one_rows = top.sb("one_rows", [3, P], BF16)
        c = Chain(top)
        b = top.sb("b", [3, H])
        cut = top.sb("cut", [3, 3, H], BF16)
        left = top.sb("left", [3, 2, H])
        sel = top.sb("sel", [3, 3, H])
        c.load(lambda e: [e.dma_start(w_attr[:, :], ins["L3_gnn_W1a"][D:D + DE, :]), e.dma_start(w_mid[:, :], ins["L3_gnn_W1b"]),
                          e.dma_start(b[:, :], ins["L3_gnn_b1b"].rearrange("(a n) -> a n", a=1).to_broadcast([3, H]))], 3)
        c.v(lambda e: [e.tensor_copy(cut[:, 0, :], b[:, :]), e.memset(one_rows[:, :], 1.0)], 2)
        c.v(lambda e: e.tensor_tensor(left[:, 0, :], b[:, :], cut[:, 0, :], ALU.subtract))
        c.v(lambda e: e.tensor_copy(cut[:, 1, :], left[:, 0, :]))
        c.v(lambda e: e.tensor_tensor(left[:, 1, :], left[:, 0, :], cut[:, 1, :], ALU.subtract))
        c.v(lambda e: e.tensor_copy(cut[:, 2, :], left[:, 1, :]))
        c.v(lambda e: [e.tensor_scalar(sel[:, a, :], cut[:, a, :], self.ident[0:3, a:a + 1], None, ALU.mult) for a in range(3)], 3)
        c.v(lambda e: e.tensor_tensor(sel[:, 0, :], sel[:, 0, :], sel[:, 1, :], ALU.add))
        c.v(lambda e: e.tensor_tensor(sel[:, 0, :], sel[:, 0, :], sel[:, 2, :], ALU.add))
        c.v(lambda e: e.tensor_copy(b_rows[:, :, :], sel[:, 0, :].unsqueeze(1).to_broadcast([3, QT, H])))
        top.run(keep=True)
        out, last = self.dram("out3", (EP, H)), self.dram("last3", (T, H))
        self.edge_pass("e3", "attr", 0, table, out, last, ch=H, weights=(w_attr, w_mid, b_rows, one_rows))
        top.stack.close()
        self.finish_sums("f3", 0, out, last, H)

        both = self.sb("both3", [P, NT, H])
        ph = Phase(self.nc, "b3c")
        c = Chain(ph)
        agg = ph.sb("agg", [P, NT, H])
        w, bias = ph.sb("w", [H, D]), ph.sb("bias", [P, D])
        inv, some = ph.sb("inv", [P, NT]), ph.sb("some", [P, NT])
        bias_n = [ph.sb(f"bias_n{k}", [P, 2, D]) for k in range(2)]
        c.g(lambda e: e.memset(agg[:, :, :], 0.0))
        self.collect(c, agg, 0, out)
        c.load(lambda e: [e.dma_start(w[:, :], ins["L3_gnn_W1c"]), e.dma_start(bias[:, :], self.broadcast_row(ins["L3_gnn_b1c"], D))], 2)
        c.v(lambda e: [e.tensor_scalar(inv[:, :], self.count[:, 0, :], 1.0, None, ALU.max),
                       e.tensor_scalar(some[:, :], self.count[:, 0, :], 1.0, None, ALU.min),
                       e.tensor_copy(both[:, :, 0:D], self.feat[:, :, 0:D])], 3)
        c.v(lambda e: e.reciprocal(inv[:, :], inv[:, :]))

        def evac(e, t, ps):
            m, bn = both[:, t:t + 2, D:H], bias_n[t // 2 % 2]
            return [lambda: e.tensor_tensor(m, ps[:, :, :], over(inv[:, t:t + 2], D), ALU.mult),
                    lambda: e.tensor_tensor(bn[:, :, :], bias[:, :].unsqueeze(1).to_broadcast([P, 2, D]), over(some[:, t:t + 2], D), ALU.mult),
                    lambda: e.tensor_tensor(m, m, bn[:, :, :], ALU.add)]
        self.linear(ph, "lin", agg[:, :, :], w[:, :], D, evac, 3, after=c)
        ph.run()
        ph = Phase(self.nc, "b3d")
        c = Chain(ph)
        w, bias, w_u, u = ph.sb("w", [H, H]), ph.sb("bias", [P, H]), ph.sb("w_u", [P, H]), ph.sb("u", [P, 1])
        c.load(lambda e: [e.dma_start(w[:, :], ins["L3_gnn_W2a"][0:H, :]), e.dma_start(bias[:, :], self.broadcast_row(ins["L3_gnn_b2a"], H)),
                          e.dma_start(w_u[:, :], self.broadcast_row(ins["L3_gnn_W2a"][H, :], H)),
                          e.dma_start(u[:, :], self.broadcast_row(ins["L3_gnn_u"][0:1], 1))], 4)
        c.v(lambda e: e.scalar_tensor_tensor(bias[:, :], w_u[:, :], u[:, :], bias[:, :], ALU.mult, ALU.add))

        def evac(e, t, ps):
            f = self.feat[:, t:t + 2, :]
            return [lambda: e.tensor_tensor(f, ps[:, :, :], bias[:, :].unsqueeze(1).to_broadcast([P, 2, H]), ALU.add),
                    lambda: e.tensor_scalar(f, f, 0.0, None, ALU.max)]
        self.linear(ph, "lin", both[:, :, :], w[:, :], H, evac, 2, after=c)
        ph.run()
        ph = Phase(self.nc, "b3e")
        c = Chain(ph)
        w, bias = ph.sb("w", [H, D]), ph.sb("bias", [P, D])
        c.load(lambda e: [e.dma_start(w[:, :], ins["L3_gnn_W2b"]), e.dma_start(bias[:, :], self.broadcast_row(ins["L3_gnn_b2b"], D))], 2)

        def evac(e, t, ps):
            x = self.x[:, t:t + 2, :]
            return [lambda: e.tensor_tensor(x, ps[:, :, :], x, ALU.add),
                    lambda: e.tensor_tensor(x, x, bias[:, :].unsqueeze(1).to_broadcast([P, 2, D]), ALU.add)]
        wait = self.linear(ph, "lin", self.feat[:, :, :], w[:, :], D, evac, 2, after=c)
        ph.on("sync", wait)
        c.load(lambda e: e.dma_start(self.out.rearrange("(p t) c -> p t c", t=NT), self.x[:, :, :]))
        c.finish()
        ph.run()


def build(nc, ins, out, stop_after=None):
    kn = Kernel(nc, ins, out)
    kn.constants()
    for name, part in (("hist", kn.histogram), ("sort", kn.sort), ("bound", kn.boundaries), ("b0", kn.block0),
                       ("b1", kn.block1), ("b2", kn.block2), ("b3", kn.block3)):
        part()
        if stop_after == name:
            break
    return kn


def layout(inputs):
    a = {k: np.asarray(v) for k, v in inputs.items()}
    m = {"x": np.concatenate([a.pop("x"), np.zeros((NP - N, D), np.float32)])}
    pad = np.full((EP - E,), N, np.int32)
    for k in ("dst", "src"):
        m[k] = np.concatenate([a.pop(k), pad]).reshape(NG, P, GT)
    m["attr"] = np.concatenate([a.pop("edge_attr_32"), np.zeros((EP - E, DE), np.float32)]).reshape(NG, P, GT, DE)
    return {**m, **a}


def kernel(**inputs):
    import concourse.bacc as bacc
    from concourse.bass_utils import run_bass_kernel_spmd

    arrays = {f"in_{k}": v for k, v in layout(inputs).items()}
    nc = bacc.Bacc("TRN2", target_bir_lowering=False, num_devices=1)
    ins = {k[3:]: nc.dram_tensor(k, v.shape, mybir.dt.from_np(v.dtype), kind="ExternalInput").ap() for k, v in arrays.items()}
    out = nc.dram_tensor("x_out", (NP, D), F32, kind="ExternalOutput").ap()
    build(nc, ins, out)
    r = run_bass_kernel_spmd(nc, [arrays], core_ids=[0])
    return r.results[0]["x_out"][0:N]
```
